# Optimizing a Trainium2 kernel written in Bass

```python
import numpy as np
import jax
import jax.numpy as jnp

def _softmax(x, axis=-1):
    return jax.nn.softmax(x, axis=axis)

def _gelu(x):
    return jax.nn.gelu(x, approximate=True)

def _silu(x):
    return jax.nn.silu(x)

def _sigmoid(x):
    return jax.nn.sigmoid(x)

def _layernorm(x, axis=-1, eps=1e-05):
    m = jnp.mean(x, axis=axis, keepdims=True)
    v = jnp.var(x, axis=axis, keepdims=True)
    return (x - m) / jnp.sqrt(v + eps)

def _scatter_add(tgt, idx, src, axis=0):
    return tgt.at[idx].add(src)

def _segment_sum(src, seg, n):
    return jax.ops.segment_sum(src, seg, n)
kernel_name = 'mk_adj_preln_d4_adj_r2_abf3d5'

def setup_inputs(seed: int=0):
    np.random.seed(seed)
    _w = jnp.asarray

    def _rec_inputs():
        import jax
        import jax.numpy as jnp
        _gk = jax.random.key(seed)
        x = -0.0002928 + 1 * jax.random.normal(jax.random.fold_in(_gk, 1), (3327, 256), jnp.float32)
        _w = (1.0 + jnp.arange(3327, dtype=jnp.float32)) ** (-0.5)
        _w = _w / _w.mean()
        _pij = jnp.clip(0.00240457 * _w[:, None] * _w[None, :], 0.0, 1.0)
        _a = jax.random.uniform(jax.random.fold_in(_gk, 2), (3327, 3327)) < _pij
        _a = jnp.logical_or(_a, jnp.swapaxes(_a, -1, -2))
        _a = jnp.logical_or(_a, jnp.eye(3327, dtype=bool))
        _af = _a.astype(jnp.float32)
        _af = _af * jax.random.uniform(jax.random.fold_in(_gk, 3), (3327, 3327), jnp.float32, 0.05, 5.41998)
        adj = _af
        return (x, adj)
    x, adj = _rec_inputs()

    def _L0_gnn_setup():
        import jax, jax.numpy as jnp
        import numpy as np
        N = 4096
        D = 256
        EPS = 1e-12
        key = jax.random.key(seed)
        k1, k2 = jax.random.split(key)
        cur = jax.random.normal(k1, (N, D), dtype=jnp.float32)
        incidence_m = jax.random.normal(k2, (N, N), dtype=jnp.float32)
        return {'cur': cur, 'incidence_m': incidence_m}
    _L0_gnn_all = _L0_gnn_setup()
    _L0_gnn_in = {k: v for k, v in _L0_gnn_all.items() if k in ()}
    del _L0_gnn_all

    def _L1_gnn_setup():
        import jax, jax.numpy as jnp
        import numpy as np
        N = 3072
        D_IN = 256
        D_OUT = 256
        DENSITY = 0.005
        key = jax.random.key(seed)
        ks = jax.random.split(key, 12)
        x = jax.random.normal(ks[0], (N, D_IN), dtype=jnp.float32)
        adj_a = (jax.random.uniform(ks[1], (N, N)) < DENSITY).astype(jnp.float32)
        adj_b = (jax.random.uniform(ks[2], (N, N)) < DENSITY).astype(jnp.float32)
        W_sa = jax.random.normal(ks[3], (D_IN, D_OUT), dtype=jnp.float32) * (1.414 / np.sqrt(D_IN + D_OUT))
        a_sa = jax.random.normal(ks[4], (1, 2 * D_OUT), dtype=jnp.float32) * (1.414 / np.sqrt(1 + 2 * D_OUT))
        stdv = 1.0 / np.sqrt(D_OUT)
        W_gcnb = jax.random.uniform(ks[5], (D_IN, D_OUT), minval=-stdv, maxval=stdv, dtype=jnp.float32)
        b_gcnb = jax.random.uniform(ks[6], (D_OUT,), minval=-stdv, maxval=stdv, dtype=jnp.float32)
        s = 1.0 / np.sqrt(2 * D_IN)
        Wa = jax.random.uniform(ks[7], (1, 2 * D_IN), minval=-s, maxval=s, dtype=jnp.float32)
        ba = jax.random.uniform(ks[8], (1,), minval=-s, maxval=s, dtype=jnp.float32)
        Wb = jax.random.uniform(ks[9], (1, 2 * D_IN), minval=-s, maxval=s, dtype=jnp.float32)
        bb = jax.random.uniform(ks[10], (1,), minval=-s, maxval=s, dtype=jnp.float32)
        return {'x': x, 'adj_a': adj_a, 'adj_b': adj_b, 'W_sa': W_sa, 'a_sa': a_sa, 'W_gcnb': W_gcnb, 'b_gcnb': b_gcnb, 'Wa': Wa, 'ba': ba, 'Wb': Wb, 'bb': bb}
    _L1_gnn_all = _L1_gnn_setup()
    _L1_gnn_in = {k: v for k, v in _L1_gnn_all.items() if k in ('W_sa', 'a_sa', 'W_gcnb', 'b_gcnb', 'Wa', 'ba', 'Wb', 'bb')}
    del _L1_gnn_all

    def _L2_gnn_setup():
        import jax, jax.numpy as jnp
        import numpy as np
        N = 4096
        D = 256
        key = jax.random.key(seed)
        ks = jax.random.split(key, 6)
        s = 1.0 / np.sqrt(D)
        return {'x': jax.random.normal(ks[0], (N, D), jnp.float32), 'spatial_encoding': jax.random.normal(ks[1], (N, N), jnp.float32), 'edge_encoding': jax.random.normal(ks[2], (N, N), jnp.float32), 'Wq': jax.random.normal(ks[3], (D, D), jnp.float32) * s, 'bq': jnp.zeros((D,), jnp.float32), 'Wk': jax.random.normal(ks[4], (D, D), jnp.float32) * s, 'bk': jnp.zeros((D,), jnp.float32), 'Wv': jax.random.normal(ks[5], (D, D), jnp.float32) * s, 'bv': jnp.zeros((D,), jnp.float32)}
    _L2_gnn_all = _L2_gnn_setup()
    _L2_gnn_in = {k: v for k, v in _L2_gnn_all.items() if k in ('Wq', 'bq', 'Wk', 'bk', 'Wv', 'bv')}
    del _L2_gnn_all

    def _L3_gnn_setup():
        import jax, jax.numpy as jnp
        import numpy as np
        N = 4096
        D = 256
        L = 2
        NEG_SLOPE = 0.01

        def _gat_layer(x, W, adj):
            proj = x @ W
            Wh, Ws = jnp.split(proj, 2, axis=-1)
            scores = Wh @ Ws.T
            a = jax.nn.softmax(scores, axis=-1) * adj
            out = a @ Wh
            out = out + x
            return jax.nn.leaky_relu(out, NEG_SLOPE)
        key = jax.random.key(seed)
        k1, k2, k3 = jax.random.split(key, 3)
        inputs = jax.random.normal(k1, (N, D), dtype=jnp.float32)
        adj = jax.random.randint(k2, (N, N), 0, 2).astype(jnp.float32)
        W_stack = jax.random.normal(k3, (L, D, 2 * D), dtype=jnp.float32) * (1.0 / np.sqrt(D))
        return {'inputs': inputs, 'adj': adj, 'W_stack': W_stack}
    _L3_gnn_all = _L3_gnn_setup()
    _L3_gnn_in = {k: v for k, v in _L3_gnn_all.items() if k in ('W_stack',)}
    del _L3_gnn_all
    return {'x': x, 'adj': adj, 'L1_gnn_W_sa': _L1_gnn_in['W_sa'], 'L1_gnn_a_sa': _L1_gnn_in['a_sa'], 'L1_gnn_W_gcnb': _L1_gnn_in['W_gcnb'], 'L1_gnn_b_gcnb': _L1_gnn_in['b_gcnb'], 'L1_gnn_Wa': _L1_gnn_in['Wa'], 'L1_gnn_ba': _L1_gnn_in['ba'], 'L1_gnn_Wb': _L1_gnn_in['Wb'], 'L1_gnn_bb': _L1_gnn_in['bb'], 'L2_gnn_Wq': _L2_gnn_in['Wq'], 'L2_gnn_bq': _L2_gnn_in['bq'], 'L2_gnn_Wk': _L2_gnn_in['Wk'], 'L2_gnn_bk': _L2_gnn_in['bk'], 'L2_gnn_Wv': _L2_gnn_in['Wv'], 'L2_gnn_bv': _L2_gnn_in['bv'], 'L3_gnn_W_stack': _L3_gnn_in['W_stack']}

def reference(x, adj, L1_gnn_W_sa, L1_gnn_a_sa, L1_gnn_W_gcnb, L1_gnn_b_gcnb, L1_gnn_Wa, L1_gnn_ba, L1_gnn_Wb, L1_gnn_bb, L2_gnn_Wq, L2_gnn_bq, L2_gnn_Wk, L2_gnn_bk, L2_gnn_Wv, L2_gnn_bv, L3_gnn_W_stack):
    import jax
    import jax.numpy as jnp

    def _L0_gnn_ref(cur, incidence_m):
        import jax, jax.numpy as jnp
        import numpy as np
        N = 4096
        D = 256
        EPS = 1e-12
        mask = incidence_m > 0
        head = jax.lax.stop_gradient(mask.astype(incidence_m.dtype))
        head = head / jnp.maximum(jnp.sqrt(jnp.sum(head * head, axis=-1, keepdims=True)), EPS)
        inc = incidence_m + head
        edge_fea = inc @ cur
        edge_degree = jnp.sum(inc, axis=-1, keepdims=True)
        return edge_fea / edge_degree

    def _L1_gnn_ref(x, adj_a, adj_b, W_sa, a_sa, W_gcnb, b_gcnb, Wa, ba, Wb, bb):
        import jax, jax.numpy as jnp
        import numpy as np
        N = 3072
        D_IN = 256
        D_OUT = 256
        DENSITY = 0.005
        type_sum_a = adj_a @ x
        type_sum_b = adj_b @ x
        attn_a = jax.nn.sigmoid(jnp.concatenate([type_sum_a, x], axis=1) @ Wa.T + ba)
        attn_b = jax.nn.sigmoid(jnp.concatenate([type_sum_b, x], axis=1) @ Wb.T + bb)
        h = x @ W_sa
        Hd = h.shape[1]
        s_left = h @ a_sa[0, :Hd]
        s_right = h @ a_sa[0, Hd:]
        scores = s_left[:, None] + s_right[None, :]
        e = jnp.where(adj_a != 0, jnp.exp(-jax.nn.leaky_relu(scores, 0.01)), 0.0)
        attn = e / (jnp.sum(e, axis=1, keepdims=True) + 1e-05)
        x_a = attn @ h
        x_b = adj_b @ (x @ W_gcnb) + b_gcnb
        return jax.nn.sigmoid(attn_a * x_a + attn_b * x_b)

    def _L2_gnn_ref(x, spatial_encoding, edge_encoding, Wq, bq, Wk, bk, Wv, bv):
        import jax, jax.numpy as jnp
        import numpy as np
        N = 4096
        D = 256
        q = x @ Wq.T + bq
        k = x @ Wk.T + bk
        v = x @ Wv.T + bv
        scale = 1.0 / jnp.sqrt(jnp.asarray(q.shape[-1], q.dtype))
        a = q @ k.T * scale + spatial_encoding + edge_encoding
        attn = jax.nn.softmax(a, axis=-1)
        return attn @ v

    def _L3_gnn_ref(inputs, adj, W_stack):
        import jax, jax.numpy as jnp
        import numpy as np
        N = 4096
        D = 256
        L = 2
        NEG_SLOPE = 0.01

        def _gat_layer(x, W, adj):
            proj = x @ W
            Wh, Ws = jnp.split(proj, 2, axis=-1)
            scores = Wh @ Ws.T
            a = jax.nn.softmax(scores, axis=-1) * adj
            out = a @ Wh
            out = out + x
            return jax.nn.leaky_relu(out, NEG_SLOPE)
        x = inputs
        for l in range(W_stack.shape[0]):
            x = _gat_layer(x, W_stack[l], adj)
        return x
    h = jnp.maximum(_layernorm(x, axis=-1), 0.0)
    x = x + _L0_gnn_ref(h, adj)
    h = jnp.maximum(_layernorm(x, axis=-1), 0.0)
    x = x + _L1_gnn_ref(h, adj, adj, L1_gnn_W_sa, L1_gnn_a_sa, L1_gnn_W_gcnb, L1_gnn_b_gcnb, L1_gnn_Wa, L1_gnn_ba, L1_gnn_Wb, L1_gnn_bb)
    h = jnp.maximum(_layernorm(x, axis=-1), 0.0)
    x = x + _L2_gnn_ref(h, adj, adj, L2_gnn_Wq, L2_gnn_bq, L2_gnn_Wk, L2_gnn_bk, L2_gnn_Wv, L2_gnn_bv)
    h = jnp.maximum(_layernorm(x, axis=-1), 0.0)
    x = x + _L3_gnn_ref(h, adj, L3_gnn_W_stack)
    return x

_drawn_inputs = setup_inputs


def setup_inputs(seed=0):
    import zlib

    import numpy as np

    out = dict(_drawn_inputs(seed))
    spreads = {'L2_gnn_bq': (0.0, 0.781), 'L2_gnn_bk': (0.0, 2.0), 'L2_gnn_bv': (0.0, 0.1)}
    factors = {'L1_gnn_W_sa': 4.031, 'L1_gnn_a_sa': 8.0, 'L1_gnn_b_gcnb': 43.302}
    for name, (base, spread) in spreads.items():
        noise = np.random.default_rng([zlib.crc32(name.encode()), seed]).standard_normal(out[name].shape)
        drawn = base * np.exp(spread * noise) if base else spread * noise
        out[name] = jnp.asarray(drawn.astype(out[name].dtype))
    for name, factor in factors.items():
        out[name] = (out[name] * factor).astype(out[name].dtype)
    return out
```

```python
from contextlib import ExitStack

import concourse.bass as bass
from concourse import mybir

P = 128
D = 256
DC = D // P
N = 3327
NB = -(-N // P)
NP = NB * P
CW = 512
NCH = -(-NP // CW)
GSTEPS = 2 * NCH
LN_EPS = 1e-5
SIGMOID_FROM = -87.0
LOW = -3.0e38

F32 = mybir.dt.float32
F32R = mybir.dt.float32r
ALU = mybir.AluOpType
ACT = mybir.ActivationFunctionType
AX = mybir.AxisListType

SCORES_AT = [(0, 1), (2, 3), (4,), (5,), (6,), (), ()]
assert [c for cs in SCORES_AT for c in cs] == list(range(NCH))


def width(c):
    return min(CW, NP - c * CW)


def live(c):
    return min(CW, N - c * CW)


def cols(c, w):
    return slice(c * CW, c * CW + w)


def wait_past(engine, semaphore, value):
    if isinstance(value, int) and value <= 0:
        return
    engine.wait_ge(semaphore, value)


def blocks(engine, slot):
    pairs = NB // 2
    for k in range(2):
        slot(0, k)
    with engine.Fori(1, pairs - 1) as half:
        for k in range(2):
            slot(half, k)
    for k in range(2):
        slot(pairs - 1, k)


def following(half, k):
    return (half, 1) if k == 0 else (half + 1, 0)


def is_last(half, k):
    return isinstance(half, int) and 2 * half + k == NB - 1


def graph_layers(nc, x, adj, eye, w_sa, a_sa, w_gcnb, b_gcnb, gate_w, gate_b, w_q, w_k, w_v, b_q, b_k,
                 b_v, w_stack, out):
    with ExitStack() as ctx:
        def sb(name, shape, dt=F32):
            return ctx.enter_context(nc.sbuf_tensor(name, shape, dt))

        def sem(name):
            return ctx.enter_context(nc.semaphore(name))

        def sems(name):
            return [sem(f"{name}{k}") for k in range(2)]

        ps = ctx.enter_context(nc.psum_tensor("ps", [P, 8, CW], F32))
        score_ps = [ps[:, k, :] for k in range(2)]
        turn_ps = [ps[:, 2 + k, :] for k in range(2)]
        sum_ps = [ps[:, 4 + k, :] for k in range(2)]
        small_ps = ps[:, 6, 0:D]
        turned_h_ps = ps[:, 7, 0:D]
        mix_ps = ps[:, 7, :]
        prep_a_ps = [ps[:, 6, 0:D], ps[:, 0, 0:D]]
        prep_b_ps = [ps[:, 7, :], ps[:, 1, :]]

        values = sb("values", [P, NB, 2, D], F32R)
        keys = sb("keys", [P, DC, 2, NP], F32R)
        values2 = keys[:].rearrange("p a b n -> p (a b n)").rearrange("p (j s d) -> p j s d", s=2, d=D)
        row_in = [sb(f"row_in{k}", [P, NP]) for k in range(2)]
        row = [sb(f"row{k}", [P, NP]) for k in range(2)]
        s_right = sb("s_right", [P, NP])
        s_left = sb("s_left", [P, NB, 2])
        turned_hi = [sb(f"turned_hi{k}", [P, CW], F32R) for k in range(2)]
        turned_lo = [sb(f"turned_lo{k}", [P, CW], F32R) for k in range(2)]
        query_hi = [sb(f"query_hi{k}", [P, DC, P], F32R) for k in range(2)]
        query_lo = [sb(f"query_lo{k}", [P, DC, P], F32R) for k in range(2)]
        weights = sb("weights", [P, DC, 3 * D])
        ident = sb("ident", [P, P])
        ht_in = [sb(f"ht_in{k}", [P, DC, P]) for k in range(2)]
        base = [sb(f"base{k}", [P, D]) for k in range(2)]
        side = [sb(f"side{k}", [P, D]) for k in range(2)]
        side2 = [sb(f"side2{k}", [P, D]) for k in range(2)]
        new_x = [sb(f"new_x{k}", [P, D]) for k in range(2)]
        new_h = [sb(f"new_h{k}", [P, D]) for k in range(2)]
        new_ht = [sb(f"new_ht{k}", [P, DC, P]) for k in range(2)]
        stat = [sb(f"stat{k}", [P, 40]) for k in range(2)]
        part = [sb(f"part{k}", [P, 2, NCH]) for k in range(2)]
        spare = [sb(f"spare{k}", [P, NCH + 1]) for k in range(2)]
        minus_half = sb("minus_half", [P, 1])
        plus_half = sb("plus_half", [P, 1])
        bias_row = sb("bias_row", [P, D])
        bias_col = sb("bias_col", [P, 2, DC])
        gate_cols = sb("gate_cols", [P, 2, 4])
        gate_bias = sb("gate_bias", [P, 2])
        fold = [sb(f"fold{k}", [P, DC, P]) for k in range(2)]

        sa_cols = weights[:, :, 0:D + 1]
        mix_cols = weights[:, :, D + 1:2 * D + 3]
        right_cols = weights[:, :, 2 * D + 3:2 * D + 3 + P]

        def dram(name, shape):
            return nc.dram_tensor(name, shape, F32, kind="Internal").ap()

        x_mid = [dram(f"x_mid{n}", (NB, P, D)) for n in range(4)]
        h_mid = [dram(f"h_mid{n}", (NB, P, D)) for n in range(3)]
        ht_mid = [dram(f"ht_mid{n}", (NB, P, DC, P)) for n in range(4)]
        adj_rows = adj.rearrange("(b p) n -> b p n", p=P)

        def st(k, a, w=1):
            return stat[k][:, a:a + w]

        consts_in = sem("consts_in")
        consts_set = sem("consts_set")
        out_stored = sems("out_stored")
        shared = {name: sem(name) for name in (
            "prep_hi", "prep_lo",
            "side_done", "sums_read")}
        shared.update({name: sems(name) for name in ("adj_in", "base_in", "ht_in")})
        frame = ["ready", "turned", "hi_done", "lo_done", "multiplied",
                 "chain2"]
        normed = ["var", "rstd"]
        features = ["h_done", "h_turned", "h_out"]
        attention = ["wts_in", "prep_mm", "query_mm", "query_hi", "query_lo",
                     "score_mm", "score_out", "top", "exp_done", "chain"]
        own_pairs = [["stored"], ["stored"], ["stored"], ["stored"], ["extra_in"]]
        own = [
            normed + features + ["prep_var", "prep_rstd", "prep_h", "prep_chain", "raw_done", "count_done",
                                 "inverse", "root", "chain"],
            normed + features + ["wts_in", "wts_set", "prep_mm", "prep_chain", "raw_done", "arg_done",
                                 "exp_done", "left_here", "ts_done", "ts_turned", "ts_out", "mix_mm", "gate_arg",
                                 "gate_exp", "sig_arg", "sig_exp"],
            normed + features + attention + ["prep_fold", "query_fold"],
            features + attention,
            ["h_out"] + attention,
        ]
        phases = []
        for n in range(5):
            named = {name: sem(f"{name}_{n}") for name in frame + own[n]}
            named.update({name: sems(f"{name}_{n}_") for name in ["prep_in"] + own_pairs[n]})
            phases.append({**shared, **named, "layer": n, "block0": NB * n, "half0": NB // 2 * n,
                           "half1": NB // 2 * (n - 1)})

        block = ctx.enter_context(nc.Block())

        def alone(engine):
            engine.wait_ge(consts_in, 16)

        @block.sync
        def _(sp):
            sp.dma_start(ident[:], eye).then_inc(consts_in, 16)

            def at(array, b):
                if isinstance(b, int):
                    return array[b]
                view = array[bass.ds(b, 1)]
                names = " ".join("cde"[:len(array.shape) - 2])
                return view.rearrange(f"o p {names} -> (o p) {names}")

            def prep_loads(n, sources):
                s = phases[n]
                for k in range(2):
                    sp.dma_start(row_in[k][:], adj_rows[k]).then_inc(s["adj_in"][k], 16)

                def slot(half, k):
                    wait_past(sp, s["prep_lo"], 2 * half + k - 1 + s["block0"])
                    for tile, array in sources:
                        sp.dma_start(tile[k][:], at(array, 2 * half + k)).then_inc(s["prep_in"][k], 16)

                blocks(sp, slot)

            def layer_loads(n, base_from, ht_from, stores, adj_freed, adj_per, extra_from=None):
                s = phases[n]

                def load_adj(half, k):
                    sp.wait_ge(adj_freed(s), adj_per * (2 * half + k - 1))
                    sp.dma_start(row_in[k][:], at(adj_rows, 2 * half + k)).then_inc(s["adj_in"][k], 16)

                def load_ht(half, k):
                    if n in (2, 3, 4):
                        wait_past(sp, s["query_mm"], 2 * half + k - 1)
                    else:
                        wait_past(sp, s["mix_mm"], 2 * half + k - 1)
                    sp.dma_start(ht_in[k][:], at(ht_from, 2 * half + k)).then_inc(s["ht_in"][k], 16)

                def store(half, k):
                    b = 2 * half + k
                    sp.wait_ge(s["h_out"], b + 1)
                    if n == 4:
                        sp.dma_start(at(out, b), new_x[k][:]).then_inc(out_stored[k], 16)
                        return
                    for tile, array in stores:
                        sp.dma_start(at(array, b), tile[k][:]).then_inc(s["stored"][k], 16)

                sp.wait_ge(s["prep_lo"], NB + s["block0"])
                for k in range(2):
                    if ht_from is not None:
                        load_ht(0, k)

                def slot(half, k):
                    b = 2 * half + k
                    wait_past(sp, s["h_out"], b - 1)
                    sp.dma_start(base[k][:], at(base_from, b)).then_inc(s["base_in"][k], 16)
                    if extra_from is not None:
                        sp.dma_start(side2[k][:], at(extra_from, b)).then_inc(s["extra_in"][k], 16)
                    if not (isinstance(half, int) and half == NB // 2 - 1):
                        if ht_from is not None:
                            load_ht(half + 1, k)
                        load_adj(half + 1, k)
                    if isinstance(half, int) and b == 0:
                        return
                    prev = (half, 0) if k == 1 else (half - 1, 1)
                    store(*prev)

                blocks(sp, slot)
                store(NB // 2 - 1, 1)
                if n < 4:
                    for k in range(2):
                        sp.wait_ge(s["stored"][k], 16 * len(stores) * (NB // 2))

            prep_loads(0, [(base, x)])
            layer_loads(0, x, None, [(new_x, x_mid[0]), (new_h, h_mid[0]), (new_ht, ht_mid[0])],
                        lambda s: s["ready"], NCH)

            s = phases[1]
            rows_of = "(c p) n -> p c n"
            sp.dma_start(weights[:, :, 0:D], w_sa.rearrange(rows_of, p=P)).then_inc(s["wts_in"], 16)
            sp.dma_start(weights[:, :, D + 1:2 * D + 1], w_gcnb.rearrange(rows_of, p=P)).then_inc(s["wts_in"], 16)
            sp.dma_start(side[0][:], a_sa[:, 0:D]).then_inc(s["wts_in"], 16)
            sp.dma_start(side[1][:], a_sa[:, D:2 * D]).then_inc(s["wts_in"], 16)
            sp.dma_start(bias_row[:], b_gcnb).then_inc(s["wts_in"], 16)
            sp.dma_start(gate_cols[:], gate_w).then_inc(s["wts_in"], 16)
            sp.dma_start(gate_bias[:], gate_b).then_inc(s["wts_in"], 16)
            prep_loads(1, [(base, h_mid[0]), (ht_in, ht_mid[0])])
            layer_loads(1, x_mid[0], ht_mid[0], [(new_x, x_mid[1]), (new_ht, ht_mid[1])],
                        lambda s: s["turned"], GSTEPS)

            s = phases[2]
            for i, w in enumerate((w_q, w_k, w_v)):
                sp.dma_start(weights[:, :, i * D:(i + 1) * D], w.rearrange(rows_of, p=P)).then_inc(s["wts_in"], 16)
            sp.dma_start(bias_row[:], b_v).then_inc(s["wts_in"], 16)
            sp.dma_start(bias_col[:, 0, :], b_q).then_inc(s["wts_in"], 16)
            sp.dma_start(bias_col[:, 1, :], b_k).then_inc(s["wts_in"], 16)
            prep_loads(2, [(ht_in, ht_mid[1])])
            layer_loads(2, x_mid[1], ht_mid[1], [(new_x, x_mid[2]), (new_h, h_mid[1]), (new_ht, ht_mid[2])],
                        lambda s: s["score_out"], NCH)

            for n in (3, 4):
                s = phases[n]
                w = w_stack[n - 3].rearrange(rows_of, p=P)
                sp.dma_start(weights[:, :, 0:2 * D], w).then_inc(s["wts_in"], 16)
                prep_loads(n, [(ht_in, ht_mid[n - 1])])
                if n == 3:
                    layer_loads(3, h_mid[1], ht_mid[2], [(new_x, h_mid[2]), (new_ht, ht_mid[3])],
                                lambda s: s["ready"], NCH)
                else:
                    layer_loads(4, h_mid[2], ht_mid[3], [], lambda s: s["ready"], NCH, extra_from=x_mid[2])
            for k in range(2):
                sp.wait_ge(out_stored[k], 16 * (NB // 2))

        @block.tensor
        def _(pe):
            pe.wait_ge(consts_in, 16)

            def turn(s, src, g, c, source_ready):
                value, j = g
                wait_past(pe, s["lo_done"], value - 1)
                source_ready()
                for i in range(width(c) // P):
                    mm = pe.transpose(turn_ps[j][:, i * P:(i + 1) * P], src[:, c * CW + i * P:c * CW + (i + 1) * P],
                                      ident[:])
                mm.then_inc(s["turned"], 1)

            def multiply(s, bank, vals, g, c):
                value, j = g
                pe.wait_ge(s["lo_done"], value + 1)
                for i in range(width(c) // P):
                    jb = c * (CW // P) + i
                    pe.matmul(bank, turned_hi[j][:, i * P:(i + 1) * P],
                              vals[:, jb, :, :].rearrange("p s d -> p (s d)"),
                              start=(jb == 0), stop=False, skip_group_check=True)
                    mm = pe.matmul(bank[:, 0:D], turned_lo[j][:, i * P:(i + 1) * P], vals[:, jb, 0, :],
                                   start=False, stop=(jb == NB - 1), skip_group_check=True)
                mm.then_inc(s["multiplied"], 1)

            def turn_h(s, half, k):
                pe.wait_ge(s["h_done"], 2 * half + k + 1)
                src = new_x[k] if s["layer"] == 3 else new_h[k]
                for i in range(DC):
                    mm = pe.transpose(turned_h_ps[:, i * P:(i + 1) * P], src[:, i * P:(i + 1) * P], ident[:])
                mm.then_inc(s["h_turned"], 1)

            def previous(half, k):
                return (half, 0) if k == 1 else (half - 1, 1)

            s = phases[0]
            pe.wait_ge(s["prep_lo"], NB + s["block0"])

            def layer0(half, k):
                b = 2 * half + k

                def count(c):
                    return NCH * b + c, (NCH * k + c) % 2

                def ready(c):
                    return lambda: pe.wait_ge(s["ready"], NCH * b + c + 1)

                turn(s, row[k], count(0), 0, ready(0))
                wait_past(pe, s["sums_read"], b - 1 + s["block0"])
                for c in range(NCH):
                    if c + 1 < NCH:
                        turn(s, row[k], count(c + 1), c + 1, ready(c + 1))
                    multiply(s, sum_ps[k], values, count(c), c)
                    if c == 4 and not (isinstance(half, int) and b == 0):
                        turn_h(s, *previous(half, k))

            blocks(pe, layer0)
            turn_h(s, NB // 2 - 1, 1)

            s = phases[1]
            pe.wait_ge(s["wts_set"], 1)

            def prep1(half, k):
                b = 2 * half + k
                pe.wait_ge(s["prep_in"][k], 32 * (half + 1))
                wait_past(pe, s["prep_lo"], b - 1 + s["block0"])
                for i in range(DC):
                    pe.matmul(prep_b_ps[k][:, 0:D + 1], ht_in[k][:, i, :], sa_cols[:, i, :], start=(i == 0),
                              stop=(i == DC - 1))
                for i in range(DC):
                    mm = pe.matmul(prep_a_ps[k][:, 0:P], right_cols[:, i, :], ht_in[k][:, i, :],
                                   start=(i == 0), stop=(i == DC - 1))
                mm.then_inc(s["prep_mm"], 1)

            blocks(pe, prep1)
            pe.wait_ge(s["prep_lo"], NB + s["block0"])

            def layer1(half, k):
                b = 2 * half + k

                def count(g):
                    return GSTEPS * b + g, g % 2

                def turn_step(g):
                    if g < NCH:
                        turn(s, row_in[k], count(g), g, lambda: pe.wait_ge(s["adj_in"][k], 16 * (half + 1 + s["half0"])))
                    else:
                        turn(s, row[k], count(g), g - NCH, lambda: pe.wait_ge(s["ready"], NCH * b + g - NCH + 1))

                turn_step(0)
                wait_past(pe, s["sums_read"], b - 1 + s["block0"])
                for g in range(GSTEPS):
                    if g + 1 < GSTEPS:
                        turn_step(g + 1)
                    if g < NCH:
                        multiply(s, sum_ps[k], values, count(g), g)
                    else:
                        multiply(s, score_ps[k], values2, count(g), g - NCH)
                    if not (isinstance(half, int) and b == 0):
                        if g == 3:
                            turn_ts(*previous(half, k))
                        if g == 5:
                            mix(*previous(half, k))
                        if g == 12:
                            turn_h(s, *previous(half, k))

            def turn_ts(half, k):
                pe.wait_ge(s["ts_done"], 2 * half + k + 1)
                for i in range(DC):
                    mm = pe.transpose(small_ps[:, i * P:(i + 1) * P], side2[k][:, i * P:(i + 1) * P], ident[:])
                mm.then_inc(s["ts_turned"], 1)

            def mix(half, k):
                pe.wait_ge(s["ts_out"], 2 * half + k + 1)
                pe.wait_ge(s["ht_in"][k], 16 * (half + 1 + s["half1"]))
                for i in range(DC):
                    pe.matmul(mix_ps[:, 0:D + 2], fold[k][:, i, :], mix_cols[:, i, :], start=(i == 0), stop=False,
                              skip_group_check=True)
                for i in range(DC):
                    mm = pe.matmul(mix_ps[:, D:D + 2], ht_in[k][:, i, :], gate_cols[:, :, 2 + i], start=False,
                                   stop=(i == DC - 1), skip_group_check=True)
                mm.then_inc(s["mix_mm"], 1)

            blocks(pe, layer1)
            turn_ts(NB // 2 - 1, 1)
            mix(NB // 2 - 1, 1)
            turn_h(s, NB // 2 - 1, 1)

            for n in (2, 3, 4):
                s = phases[n]
                key_at = D
                value_at = 2 * D if n == 2 else 0
                pe.wait_ge(s["wts_in"], 16 * (6 if n == 2 else 1))

                def prep(half, k):
                    b = 2 * half + k
                    pe.wait_ge(s["prep_in"][k], 16 * (half + 1))
                    wait_past(pe, s["prep_lo"], b - 1 + s["block0"])
                    for o in range(DC):
                        for i in range(DC):
                            pe.matmul(prep_a_ps[k][:, o * P:(o + 1) * P],
                                      weights[:, i, key_at + o * P:key_at + (o + 1) * P], ht_in[k][:, i, :],
                                      start=(i == 0), stop=(i == DC - 1))
                    for i in range(DC):
                        mm = pe.matmul(prep_b_ps[k][:, 0:D], ht_in[k][:, i, :],
                                       weights[:, i, value_at:value_at + D], start=(i == 0), stop=(i == DC - 1))
                    mm.then_inc(s["prep_mm"], 1)

                blocks(pe, prep)
                pe.wait_ge(s["prep_lo"], NB + s["block0"])

                def query(half, k):
                    b = 2 * half + k
                    pe.wait_ge(s["ht_in"][k], 16 * (half + 1 + s["half1"]))
                    wait_past(pe, s["query_lo"], b)
                    for o in range(DC):
                        for i in range(DC):
                            mm = pe.matmul(small_ps[:, o * P:(o + 1) * P], weights[:, i, o * P:(o + 1) * P],
                                           ht_in[k][:, i, :], start=(i == 0), stop=(i == DC - 1))
                    mm.then_inc(s["query_mm"], 1)

                def scores(half, k, c):
                    b = 2 * half + k
                    j = (NCH * k + c) % 2
                    pe.wait_ge(s["query_lo"], b + 1)
                    wait_past(pe, s["score_out"], NCH * b + c - 1)
                    w = width(c)
                    for i in range(DC):
                        for q, side_of_key in ((query_hi, 0), (query_hi, 1), (query_lo, 0)):
                            mm = pe.matmul(score_ps[j][:, 0:w], q[k][:, i, :], keys[:, i, side_of_key, cols(c, w)],
                                           start=(i == 0 and q is query_hi and side_of_key == 0),
                                           stop=(i == DC - 1 and q is query_lo))
                    mm.then_inc(s["score_mm"], 1)

                query(0, 0)
                query(0, 1)
                for c in range(NCH):
                    scores(0, 0, c)

                def attend(half, k):
                    b = 2 * half + k

                    def count(c):
                        return NCH * b + c, (NCH * k + c) % 2

                    def ready(c):
                        return lambda: pe.wait_ge(s["ready"], NCH * b + c + 1)

                    for c in range(NCH):
                        if not is_last(half, k):
                            for a in SCORES_AT[c]:
                                scores(*following(half, k), a)
                        if c == 0:
                            turn(s, row[k], count(0), 0, ready(0))
                            wait_past(pe, s["sums_read"], b - 1 + s["block0"])
                        if c + 1 < NCH:
                            turn(s, row[k], count(c + 1), c + 1, ready(c + 1))
                        multiply(s, sum_ps[k], values, count(c), c)
                        if c == 4 and not (isinstance(half, int) and b == 0) and n < 4:
                            turn_h(s, *previous(half, k))
                        if c == 5 and not (isinstance(half, int) and half == NB // 2 - 1):
                            query(half + 1, k)

                blocks(pe, attend)
                if n < 4:
                    turn_h(s, NB // 2 - 1, 1)

        @block.scalar
        def _(act):
            def hi_part(s, g, c):
                value, j = g
                act.wait_ge(s["turned"], value + 1)
                wait_past(act, s["multiplied"], value - 1)
                act.activation(turned_hi[j][:, 0:width(c)], turn_ps[j][:, 0:width(c)], ACT.Copy)\
                   .then_inc(s["hi_done"], 1)

            def side_copy(s, half, k):
                b = 2 * half + k
                steps = GSTEPS if s["layer"] == 1 else NCH
                act.wait_ge(s["multiplied"], steps * (b + 1))
                wait_past(act, s["sums_read"], b - 1 + s["block0"])
                if s["layer"] == 1:
                    act.activation(new_h[k][:], score_ps[k][:, D:2 * D], ACT.Copy)
                act.activation(side[k][:], sum_ps[k][:, D:2 * D], ACT.Copy).then_inc(s["side_done"], 1)

            def ht_copy(s, half, k):
                b = 2 * half + k
                act.wait_ge(s["h_turned"], b + 1)
                stores = {0: 3, 1: 2, 2: 3, 3: 2}[s["layer"]]
                wait_past(act, s["stored"][k], 16 * stores * half)
                act.activation(new_ht[k][:].rearrange("p c n -> p (c n)"), turned_h_ps, ACT.Copy)\
                   .then_inc(s["h_out"], 1)

            def previous(half, k):
                return (half, 0) if k == 1 else (half - 1, 1)

            s = phases[0]

            def prep0(half, k):
                b = 2 * half + k
                act.wait_ge(s["prep_h"], b + 1)
                alone(act)
                act.activation(values[:, bass.ds(b, 1), 0, :].rearrange("p o d -> p (o d)"), new_h[k][:],
                               ACT.Copy).then_inc(s["prep_hi"], 1)

            blocks(act, prep0)

            def sign(half, k, c):
                b = 2 * half + k
                act.wait_ge(s["adj_in"][k], 16 * (half + 1 + s["half0"]))
                wait_past(act, s["turned"], NCH * (b - 2) + c + 1)
                act.activation(row[k][:, cols(c, width(c))], row_in[k][:, cols(c, width(c))], ACT.Relu)\
                   .then_inc(s["raw_done"], 1)
                act.wait_ge(s["raw_done"], NCH * b + c + 1)
                act.activation(row[k][:, cols(c, width(c))], row[k][:, cols(c, width(c))], ACT.Sign,
                               accum_out=part[k][:, 0, c:c + 1]).then_inc(s["count_done"], 1)

            for c in range(NCH):
                sign(0, 0, c)

            def layer0(half, k):
                b = 2 * half + k
                for c in range(NCH):
                    hi_part(s, (NCH * b + c, (NCH * k + c) % 2), c)
                    if not is_last(half, k):
                        sign(*following(half, k), c)
                    if not (isinstance(half, int) and b == 0):
                        if c == 0:
                            side_copy(s, *previous(half, k))
                        if c == 5:
                            ht_copy(s, *previous(half, k))

            blocks(act, layer0)
            side_copy(s, NB // 2 - 1, 1)
            ht_copy(s, NB // 2 - 1, 1)

            s = phases[1]

            def prep1(half, k):
                b = 2 * half + k
                act.wait_ge(s["prep_in"][k], 32 * (half + 1))
                alone(act)
                act.activation(values[:, bass.ds(b, 1), 0, :].rearrange("p o d -> p (o d)"), base[k][:], ACT.Copy)
                act.wait_ge(s["prep_mm"], b + 1)
                alone(act)
                act.activation(s_right[:, bass.ds(b * P, P)], prep_a_ps[k][:, 0:P], ACT.Copy)
                act.activation(values2[:, bass.ds(b, 1), 0, :].rearrange("p o d -> p (o d)"),
                               prep_b_ps[k][:, 0:D], ACT.Copy).then_inc(s["prep_hi"], 1)

            blocks(act, prep1)
            act.wait_ge(s["prep_lo"], NB + s["block0"])

            def positive_part(half, k, c):
                b = 2 * half + k
                if c == 0:
                    act.wait_ge(s["left_here"], b + 1)
                wait_past(act, s["turned"], GSTEPS * (b - 2) + NCH + c + 1)
                act.activation(row[k][:, cols(c, width(c))], s_right[:, cols(c, width(c))], ACT.Relu,
                               bias=st(k, 26)).then_inc(s["raw_done"], 1)

            def exponential(half, k, c):
                b = 2 * half + k
                act.wait_ge(s["arg_done"], NCH * b + c + 1)
                act.activation(row[k][:, cols(c, width(c))], row[k][:, cols(c, width(c))], ACT.Exp,
                               bias=st(k, 27), scale=-0.01).then_inc(s["exp_done"], 1)

            for c in range(NCH):
                positive_part(0, 0, c)
            for c in range(NCH):
                exponential(0, 0, c)

            def ts_copy(half, k):
                act.wait_ge(s["ts_turned"], 2 * half + k + 1)
                act.activation(fold[k][:].rearrange("p c n -> p (c n)"), small_ps, ACT.Copy).then_inc(s["ts_out"], 1)

            def gate_exp(half, k):
                act.wait_ge(s["gate_arg"], 2 * half + k + 1)
                act.activation(st(k, 2, 2), st(k, 0, 2), ACT.Exp, scale=-1.0).then_inc(s["gate_exp"], 1)

            def sig_exp(half, k):
                act.wait_ge(s["sig_arg"], 2 * half + k + 1)
                act.activation(side[k][:], side2[k][:], ACT.Exp, scale=-1.0).then_inc(s["sig_exp"], 1)

            def layer1(half, k):
                b = 2 * half + k
                for g in range(GSTEPS):
                    hi_part(s, (GSTEPS * b + g, g % 2), g % NCH)
                    if not is_last(half, k):
                        if g < NCH:
                            positive_part(*following(half, k), g)
                        else:
                            exponential(*following(half, k), g - NCH)
                    if not (isinstance(half, int) and b == 0):
                        prev = previous(half, k)
                        if g == 0:
                            side_copy(s, *prev)
                        if g == 3:
                            ts_copy(*prev)
                        if g == 6:
                            gate_exp(*prev)
                        if g == 8:
                            sig_exp(*prev)
                        if g == 12:
                            ht_copy(s, *prev)

            blocks(act, layer1)
            end = (NB // 2 - 1, 1)
            side_copy(s, *end)
            ts_copy(*end)
            gate_exp(*end)
            sig_exp(*end)
            ht_copy(s, *end)

            for n in (2, 3, 4):
                s = phases[n]

                def prep(half, k):
                    b = 2 * half + k
                    if n == 2:
                        act.wait_ge(s["prep_fold"], b + 1)
                        key_src = fold[k][:]
                        value_src = new_h[k][:]
                    else:
                        act.wait_ge(s["prep_mm"], b + 1)
                        key_src = prep_a_ps[k].rearrange("p (c n) -> p c n", c=DC)
                        value_src = prep_b_ps[k][:, 0:D]
                    alone(act)
                    act.activation(keys[:, :, 0, bass.ds(b * P, P)], key_src, ACT.Copy)
                    act.activation(values[:, bass.ds(b, 1), 0, :].rearrange("p o d -> p (o d)"), value_src,
                                   ACT.Copy).then_inc(s["prep_hi"], 1)

                blocks(act, prep)

                def query_hi_part(half, k):
                    b = 2 * half + k
                    wait_past(act, s["score_mm"], NCH * (b - 1))
                    if n == 2:
                        act.wait_ge(s["query_fold"], b + 1)
                        act.activation(query_hi[k][:], fold[k][:], ACT.Copy, scale=1.0 / 32)\
                           .then_inc(s["query_hi"], 1)
                    else:
                        act.wait_ge(s["query_mm"], b + 1)
                        act.activation(query_hi[k][:], small_ps.rearrange("p (c n) -> p c n", c=DC), ACT.Copy)\
                           .then_inc(s["query_hi"], 1)

                query_hi_part(0, 0)
                query_hi_part(0, 1)

                def exponential(half, k, c):
                    b = 2 * half + k
                    if c == 0:
                        act.wait_ge(s["top"], b + 1)
                    act.activation(row[k][:, cols(c, live(c))], row[k][:, cols(c, live(c))], ACT.Exp,
                                   bias=st(k, 1), accum_out=part[k][:, 1, c:c + 1])\
                       .then_inc(s["ready"] if n == 2 else s["exp_done"], 1)

                def attend(half, k):
                    b = 2 * half + k
                    exponential(half, k, 0)
                    exponential(half, k, 1)
                    for c in range(NCH):
                        if c + 2 < NCH:
                            exponential(half, k, c + 2)
                        hi_part(s, (NCH * b + c, (NCH * k + c) % 2), c)
                        if not (isinstance(half, int) and b == 0):
                            if c == 0:
                                side_copy(s, *previous(half, k))
                            if c == 4 and n < 4:
                                ht_copy(s, *previous(half, k))
                        if c == 5 and not (isinstance(half, int) and half == NB // 2 - 1):
                            query_hi_part(half + 1, k)

                blocks(act, attend)
                side_copy(s, *end)
                if n < 4:
                    ht_copy(s, *end)

        @block.vector
        def _(dve):
            nc.vector.memset(minus_half[:], -0.5).then_inc(consts_set, 1)
            nc.vector.memset(plus_half[:], 0.5).then_inc(consts_set, 1)

            def chained(semaphore, before):
                done = [0]

                def link(instruction):
                    done[0] += 1
                    instruction.then_inc(semaphore, 1)
                    dve.wait_ge(semaphore, before + done[0])

                return link

            def lo_part(s, g, c):
                value, j = g
                dve.wait_ge(s["hi_done"], value + 1)
                wait_past(dve, s["multiplied"], value - 1)
                dve.tensor_tensor(turned_lo[j][:, 0:width(c)], turn_ps[j][:, 0:width(c)],
                                  turned_hi[j][:, 0:width(c)].bitcast(F32), ALU.subtract).then_inc(s["lo_done"], 1)

            def previous(half, k):
                return (half, 0) if k == 1 else (half - 1, 1)

            def take_wait(k, column):
                dve.memset(spare[k][:, column:column + 1], 0.0)

            def variance(link, src, k, semaphore):
                link(dve.bn_stats(st(k, 4, 6), src))
                take_wait(k, NCH)
                link(dve.bn_aggr(st(k, 10, 2), st(k, 4, 6)))
                dve.tensor_scalar(st(k, 12), st(k, 11), LN_EPS, None, ALU.add).then_inc(semaphore, 1)

            def relu_norm(link, src, k, rstd_ready, semaphore):
                rstd_ready()
                link(dve.tensor_scalar(new_h[k][:], src, st(k, 10), st(k, 13), ALU.subtract, ALU.mult))
                dve.tensor_scalar(new_h[k][:], new_h[k][:], 0.0, None, ALU.max).then_inc(semaphore, 1)

            s = phases[0]

            def prep0(half, k):
                b = 2 * half + k
                dve.wait_ge(s["prep_in"][k], 16 * (half + 1))
                link = chained(s["prep_chain"], 3 * b)
                variance(link, base[k][:], k, s["prep_var"])
                relu_norm(link, base[k][:], k, lambda: dve.wait_ge(s["prep_rstd"], b + 1), s["prep_h"])
                dve.wait_ge(s["prep_hi"], b + 1 + s["block0"])
                dve.tensor_tensor(values[:, bass.ds(b, 1), 1, :].rearrange("p o d -> p (o d)"), new_h[k][:],
                                  values[:, bass.ds(b, 1), 0, :].rearrange("p o d -> p (o d)").bitcast(F32),
                                  ALU.subtract).then_inc(s["prep_lo"], 1)

            blocks(dve, prep0)

            def inverse_norm(half, k):
                b = 2 * half + k
                link = chained(s["chain"], 2 * b)
                dve.wait_ge(s["count_done"], NCH * (b + 1))
                dve.tensor_reduce(st(k, 14), part[k][:, 0, :], AX.X, ALU.add).then_inc(s["inverse"], 1)
                dve.wait_ge(s["root"], b + 1)
                link(dve.tensor_scalar(st(k, 16), st(k, 15), 1e-12, None, ALU.max))
                link(dve.reciprocal(st(k, 16), st(k, 16)))

            def incidence(half, k, c):
                w = width(c)
                dve.scalar_tensor_tensor(out=row[k][:, cols(c, w)], in0=row[k][:, cols(c, w)], scalar=st(k, 16),
                                         in1=row_in[k][:, cols(c, w)], op0=ALU.mult, op1=ALU.add,
                                         accum_out=part[k][:, 1, c:c + 1]).then_inc(s["ready"], 1)

            def epilogue0(half, k):
                b = 2 * half + k
                link = chained(s["chain2"], 6 * b)
                link(dve.tensor_reduce(st(k, 17), part[k][:, 1, :], AX.X, ALU.add))
                link(dve.reciprocal(st(k, 18), st(k, 17)))
                dve.wait_ge(s["side_done"], b + 1 + s["block0"])
                dve.wait_ge(s["base_in"][k], 16 * (half + 1 + s["half0"]))
                wait_stores(s, 3, half, k)
                dve.tensor_tensor(new_x[k][:], sum_ps[k][:, 0:D], side[k][:], ALU.add).then_inc(s["sums_read"], 1)
                dve.wait_ge(s["sums_read"], b + 1 + s["block0"])
                link(dve.scalar_tensor_tensor(out=new_x[k][:], in0=new_x[k][:], scalar=st(k, 18), in1=base[k][:],
                                              op0=ALU.mult, op1=ALU.add))
                variance(link, new_x[k][:], k, s["var"])

            def wait_stores(s, stores, half, k):
                wait_past(dve, s["stored"][k], 16 * stores * half)

            def epilogue_h(s, half, k, per):
                b = 2 * half + k
                link = chained(s["chain2"], per * b + per - 1)
                relu_norm(link, new_x[k][:], k, lambda: dve.wait_ge(s["rstd"], b + 1), s["h_done"])

            def layer0(half, k):
                b = 2 * half + k
                inverse_norm(half, k)
                incidence(half, k, 0)
                incidence(half, k, 1)
                for c in range(NCH):
                    if c + 2 < NCH:
                        incidence(half, k, c + 2)
                    lo_part(s, (NCH * b + c, (NCH * k + c) % 2), c)
                    if not (isinstance(half, int) and b == 0):
                        if c == 1:
                            epilogue0(*previous(half, k))
                        if c == 3:
                            epilogue_h(s, *previous(half, k), 6)

            end = (NB // 2 - 1, 1)
            blocks(dve, layer0)
            epilogue0(*end)
            epilogue_h(s, *end, 6)

            s = phases[1]
            dve.wait_ge(s["wts_in"], 7 * 16)
            link = chained(s["prep_chain"], 0)
            for i in range(DC):
                link(dve.tensor_tensor_reduce(row[1][:, 0:D], weights[:, i, 0:D], side[0][:], 1.0, 0.0, ALU.mult,
                                              ALU.add, sa_cols[:, i, D:D + 1]))
                link(dve.tensor_tensor_reduce(row[1][:, 0:D], weights[:, i, 0:D], side[1][:], 1.0, 0.0, ALU.mult,
                                              ALU.add, st(0, 20 + i)))
            link(dve.memset(row[1][:, 0:P], 1.0))
            for i in range(DC):
                link(dve.tensor_scalar(right_cols[:, i, :], row[1][:, 0:P], st(0, 20 + i), None, ALU.mult))
            dve.tensor_copy(mix_cols[:, :, D:D + 2], gate_cols[:, :, 0:DC].rearrange("p g c -> p c g"))\
               .then_inc(s["wts_set"], 1)

            def prep1(half, k):
                b = 2 * half + k
                dve.wait_ge(s["prep_hi"], b + 1 + s["block0"])
                dve.tensor_scalar(s_left[:, bass.ds(b, 1), 0], prep_b_ps[k][:, D:D + 1], 1.0, None, ALU.mult)
                dve.tensor_scalar(s_left[:, bass.ds(b, 1), 1], prep_b_ps[k][:, D:D + 1], -0.01, None, ALU.mult)
                dve.tensor_tensor(values[:, bass.ds(b, 1), 1, :].rearrange("p o d -> p (o d)"), base[k][:],
                                  values[:, bass.ds(b, 1), 0, :].rearrange("p o d -> p (o d)").bitcast(F32),
                                  ALU.subtract)
                dve.tensor_tensor(values2[:, bass.ds(b, 1), 1, :].rearrange("p o d -> p (o d)"),
                                  prep_b_ps[k][:, 0:D],
                                  values2[:, bass.ds(b, 1), 0, :].rearrange("p o d -> p (o d)").bitcast(F32),
                                  ALU.subtract).then_inc(s["prep_lo"], 1)

            blocks(dve, prep1)

            def argument(half, k, c):
                b = 2 * half + k
                w = width(c)
                dve.wait_ge(s["raw_done"], NCH * b + c + 1)
                dve.scalar_tensor_tensor(out=row[k][:, cols(c, w)], in0=row[k][:, cols(c, w)], scalar=99.0,
                                         in1=s_right[:, cols(c, w)], op0=ALU.mult, op1=ALU.add)\
                   .then_inc(s["arg_done"], 1)

            def masked(half, k, c):
                b = 2 * half + k
                w = width(c)
                dve.wait_ge(s["adj_in"][k], 16 * (half + 1 + s["half0"]))
                dve.wait_ge(s["exp_done"], NCH * b + c + 1)
                dve.scalar_tensor_tensor(out=row[k][:, cols(c, w)], in0=row_in[k][:, cols(c, w)], scalar=0.0,
                                         in1=row[k][:, cols(c, w)], op0=ALU.not_equal, op1=ALU.mult,
                                         accum_out=part[k][:, 0, c:c + 1]).then_inc(s["ready"], 1)

            def left(half, k):
                dve.tensor_scalar(st(k, 26, 2), s_left[:, bass.ds(2 * half + k, 1), :]
                                  .rearrange("p o t -> p (o t)"), 1.0, None, ALU.mult).then_inc(s["left_here"], 1)

            dve.wait_ge(s["prep_lo"], NB + s["block0"])
            left(0, 0)
            for c in range(NCH):
                argument(0, 0, c)
            for c in range(NCH):
                masked(0, 0, c)

            PER1 = 16

            def sums1(half, k):
                b = 2 * half + k
                link = chained(s["chain2"], PER1 * b)
                dve.wait_ge(s["side_done"], b + 1 + s["block0"])
                dve.tensor_tensor(side2[k][:], sum_ps[k][:, 0:D], side[k][:], ALU.add).then_inc(s["ts_done"], 1)
                wait_stores(s, 2, half, k)
                dve.tensor_tensor(new_x[k][:], score_ps[k][:, 0:D], new_h[k][:], ALU.add).then_inc(s["sums_read"], 1)
                link(dve.tensor_reduce(st(k, 14), part[k][:, 0, :], AX.X, ALU.add))
                link(dve.tensor_scalar(st(k, 15), st(k, 14), 1e-5, None, ALU.add))
                link(dve.reciprocal(st(k, 16), st(k, 15)))

            def gates1(half, k):
                b = 2 * half + k
                dve.wait_ge(s["mix_mm"], b + 1)
                link = chained(s["chain2"], PER1 * b + 3)
                link(dve.tensor_tensor(st(k, 0, 2), mix_ps[:, D:D + 2], gate_bias[:], ALU.add))
                dve.tensor_scalar(st(k, 0, 2), st(k, 0, 2), SIGMOID_FROM, None, ALU.max).then_inc(s["gate_arg"], 1)
                link(dve.tensor_tensor(side2[k][:], mix_ps[:, 0:D], bias_row[:], ALU.add))

            def mixed1(half, k):
                b = 2 * half + k
                link = chained(s["chain2"], PER1 * b + 5)
                dve.wait_ge(s["gate_exp"], b + 1)
                link(dve.tensor_scalar(st(k, 20, 2), st(k, 2, 2), 1.0, None, ALU.add))
                link(dve.reciprocal(st(k, 22, 2), st(k, 20, 2)))
                link(dve.tensor_tensor(st(k, 24), st(k, 22), st(k, 16), ALU.mult))
                link(dve.tensor_scalar(side2[k][:], side2[k][:], st(k, 23), None, ALU.mult))
                link(dve.scalar_tensor_tensor(out=side2[k][:], in0=new_x[k][:], scalar=st(k, 24), in1=side2[k][:],
                                              op0=ALU.mult, op1=ALU.add))
                dve.tensor_scalar(side2[k][:], side2[k][:], SIGMOID_FROM, None, ALU.max).then_inc(s["sig_arg"], 1)

            def result1(half, k):
                b = 2 * half + k
                link = chained(s["chain2"], PER1 * b + 10)
                dve.wait_ge(s["sig_exp"], b + 1)
                dve.wait_ge(s["base_in"][k], 16 * (half + 1 + s["half0"]))
                link(dve.tensor_scalar(new_x[k][:], side[k][:], 1.0, None, ALU.add))
                link(dve.reciprocal(new_x[k][:], new_x[k][:]))
                link(dve.tensor_tensor(new_x[k][:], new_x[k][:], base[k][:], ALU.add))
                variance(link, new_x[k][:], k, s["var"])

            def layer1(half, k):
                b = 2 * half + k
                if not is_last(half, k):
                    left(*following(half, k))
                for g in range(GSTEPS):
                    lo_part(s, (GSTEPS * b + g, g % 2), g % NCH)
                    if not is_last(half, k):
                        if g < NCH:
                            argument(*following(half, k), g)
                        else:
                            masked(*following(half, k), g - NCH)
                    if not (isinstance(half, int) and b == 0):
                        prev = previous(half, k)
                        if g == 1:
                            sums1(*prev)
                        if g == 6:
                            gates1(*prev)
                        if g == 7:
                            mixed1(*prev)
                        if g == 9:
                            result1(*prev)
                        if g == 11:
                            epilogue_h(s, *prev, PER1)

            blocks(dve, layer1)
            sums1(*end)
            gates1(*end)
            mixed1(*end)
            result1(*end)
            epilogue_h(s, *end, PER1)

            for n in (2, 3, 4):
                s = phases[n]
                if n == 2:
                    dve.wait_ge(s["wts_in"], 6 * 16)
                    for k in range(2):
                        dve.memset(row[k][:, N:NP], 0.0)

                def prep(half, k):
                    b = 2 * half + k
                    if n == 2:
                        dve.wait_ge(s["prep_mm"], b + 1)
                        wait_past(dve, s["prep_hi"], b - 1 + s["block0"])
                        dve.tensor_tensor(fold[k][:], prep_a_ps[k].rearrange("p (c n) -> p c n", c=DC),
                                          bias_col[:, 1, :, None].broadcast_to((P, DC, P)), ALU.add)
                        dve.tensor_tensor(new_h[k][:], prep_b_ps[k][:, 0:D], bias_row[:], ALU.add)\
                           .then_inc(s["prep_fold"], 1)
                        key_src = fold[k][:]
                        value_src = new_h[k][:]
                    else:
                        key_src = prep_a_ps[k].rearrange("p (c n) -> p c n", c=DC)
                        value_src = prep_b_ps[k][:, 0:D]
                    dve.wait_ge(s["prep_hi"], b + 1 + s["block0"])
                    dve.tensor_tensor(keys[:, :, 1, bass.ds(b * P, P)], key_src,
                                      keys[:, :, 0, bass.ds(b * P, P)].bitcast(F32), ALU.subtract)
                    dve.tensor_tensor(values[:, bass.ds(b, 1), 1, :].rearrange("p o d -> p (o d)"), value_src,
                                      values[:, bass.ds(b, 1), 0, :].rearrange("p o d -> p (o d)").bitcast(F32),
                                      ALU.subtract).then_inc(s["prep_lo"], 1)

                blocks(dve, prep)

                def query_fold_part(half, k):
                    b = 2 * half + k
                    dve.wait_ge(s["query_mm"], b + 1)
                    dve.tensor_tensor(fold[k][:], small_ps.rearrange("p (c n) -> p c n", c=DC),
                                      bias_col[:, 0, :, None].broadcast_to((P, DC, P)), ALU.add)\
                       .then_inc(s["query_fold"], 1)

                def query_lo_part(half, k):
                    b = 2 * half + k
                    dve.wait_ge(s["query_hi"], b + 1)
                    if n == 2:
                        dve.scalar_tensor_tensor(out=query_lo[k][:], in0=fold[k][:], scalar=1.0 / 32,
                                                 in1=query_hi[k][:].bitcast(F32), op0=ALU.mult,
                                                 op1=ALU.subtract).then_inc(s["query_lo"], 1)
                    else:
                        dve.tensor_tensor(query_lo[k][:], small_ps.rearrange("p (c n) -> p c n", c=DC),
                                          query_hi[k][:].bitcast(F32), ALU.subtract).then_inc(s["query_lo"], 1)

                def score_out(half, k, c):
                    b = 2 * half + k
                    j = (NCH * k + c) % 2
                    w = live(c)
                    dve.wait_ge(s["score_mm"], NCH * b + c + 1)
                    wait_past(dve, s["turned"], NCH * (b - 2) + c + 1)
                    top = part[k][:, 0, c:c + 1]
                    if n == 2:
                        dve.wait_ge(s["adj_in"][k], 16 * (half + 1 + s["half0"]))
                        take_wait(k, c)
                        dve.tensor_tensor_reduce(row[k][:, cols(c, w)], score_ps[j][:, 0:w],
                                                 row_in[k][:, cols(c, w)], 2.0, LOW, ALU.add, ALU.max, top)\
                           .then_inc(s["score_out"], 1)
                    else:
                        dve.tensor_scalar(row[k][:, cols(c, w)], score_ps[j][:, 0:w], 1.0, LOW, ALU.mult,
                                          ALU.max, accum_out=top).then_inc(s["score_out"], 1)

                def row_top(half, k):
                    b = 2 * half + k
                    dve.wait_ge(s["score_out"], NCH * (b + 1))
                    link = chained(s["chain"], b)
                    link(dve.tensor_reduce(st(k, 0), part[k][:, 0, :], AX.X, ALU.max))
                    dve.tensor_scalar(st(k, 1), st(k, 0), -1.0, None, ALU.mult).then_inc(s["top"], 1)

                def weigh(half, k, c):
                    b = 2 * half + k
                    w = live(c)
                    if n == 2:
                        return
                    dve.wait_ge(s["exp_done"], NCH * b + c + 1)
                    dve.wait_ge(s["adj_in"][k], 16 * (half + 1 + s["half0"]))
                    dve.tensor_tensor(row[k][:, cols(c, w)], row[k][:, cols(c, w)], row_in[k][:, cols(c, w)],
                                      ALU.mult).then_inc(s["ready"], 1)

                for k in range(2):
                    if n == 2:
                        query_fold_part(0, k)
                    query_lo_part(0, k)
                for c in range(NCH):
                    score_out(0, 0, c)

                def epilogue(half, k):
                    b = 2 * half + k
                    link = chained(s["chain2"], {2: 6, 3: 3, 4: 4}[n] * b)
                    link(dve.tensor_reduce(st(k, 17), part[k][:, 1, :], AX.X, ALU.add))
                    link(dve.reciprocal(st(k, 18), st(k, 17)))
                    dve.wait_ge(s["side_done"], b + 1 + s["block0"])
                    dve.wait_ge(s["base_in"][k], 16 * (half + 1 + s["half0"]))
                    if n < 4:
                        wait_stores(s, {2: 3, 3: 2}[n], half, k)
                    else:
                        wait_past(dve, out_stored[k], 16 * half)
                    dve.tensor_tensor(new_x[k][:], sum_ps[k][:, 0:D], side[k][:], ALU.add)\
                       .then_inc(s["sums_read"], 1)
                    dve.wait_ge(s["sums_read"], b + 1 + s["block0"])
                    link(dve.scalar_tensor_tensor(out=new_x[k][:], in0=new_x[k][:], scalar=st(k, 18),
                                                  in1=base[k][:], op0=ALU.mult, op1=ALU.add))
                    if n == 2:
                        variance(link, new_x[k][:], k, s["var"])
                        return
                    leaky = dve.scalar_tensor_tensor(out=new_x[k][:], in0=new_x[k][:], scalar=0.01,
                                                     in1=new_x[k][:], op0=ALU.mult, op1=ALU.max)
                    if n == 3:
                        leaky.then_inc(s["h_done"], 1)
                        return
                    link(leaky)
                    dve.wait_ge(s["extra_in"][k], 16 * (half + 1))
                    dve.tensor_tensor(new_x[k][:], new_x[k][:], side2[k][:], ALU.add).then_inc(s["h_out"], 1)

                def attend(half, k):
                    b = 2 * half + k
                    row_top(half, k)
                    weigh(half, k, 0)
                    for c in range(NCH):
                        if not is_last(half, k):
                            for a in SCORES_AT[c]:
                                score_out(*following(half, k), a)
                        if c == 0:
                            weigh(half, k, 1)
                        if c + 2 < NCH:
                            weigh(half, k, c + 2)
                        lo_part(s, (NCH * b + c, (NCH * k + c) % 2), c)
                        if not (isinstance(half, int) and b == 0):
                            if c == 1:
                                epilogue(*previous(half, k))
                            if c == 3 and n == 2:
                                epilogue_h(s, *previous(half, k), 6)
                        if c == 5 and not (isinstance(half, int) and half == NB // 2 - 1):
                            if n == 2:
                                query_fold_part(half + 1, k)
                            query_lo_part(half + 1, k)

                blocks(dve, attend)
                epilogue(*end)
                if n == 2:
                    epilogue_h(s, *end, 6)

        @block.gpsimd
        def _(pool):
            pool.wait_ge(consts_set, 2)

            def rstd(arg, done):
                def slot(half, k):
                    pool.wait_ge(arg, 2 * half + k + 1)
                    nc.gpsimd.tensor_tensor(st(k, 13), st(k, 12), minus_half[:], ALU.pow).then_inc(done, 1)

                return slot

            s = phases[0]
            blocks(pool, rstd(s["prep_var"], s["prep_rstd"]))

            def root(half, k):
                pool.wait_ge(s["inverse"], 2 * half + k + 1)
                nc.gpsimd.tensor_tensor(st(k, 15), st(k, 14), plus_half[:], ALU.pow).then_inc(s["root"], 1)

            def layer0(half, k):
                root(half, k)
                if not (isinstance(half, int) and 2 * half + k == 0):
                    rstd(s["var"], s["rstd"])(*((half, 0) if k == 1 else (half - 1, 1)))

            blocks(pool, layer0)
            rstd(s["var"], s["rstd"])(NB // 2 - 1, 1)
            for n in (1, 2):
                blocks(pool, rstd(phases[n]["var"], phases[n]["rstd"]))


def kernel(x, adj, L1_gnn_W_sa, L1_gnn_a_sa, L1_gnn_W_gcnb, L1_gnn_b_gcnb, L1_gnn_Wa, L1_gnn_ba, L1_gnn_Wb,
           L1_gnn_bb, L2_gnn_Wq, L2_gnn_bq, L2_gnn_Wk, L2_gnn_bk, L2_gnn_Wv, L2_gnn_bv, L3_gnn_W_stack):
    import numpy as np
    import concourse.bacc as bacc
    from concourse.bass_utils import run_bass_kernel_spmd

    nc = bacc.Bacc("TRN2", target_bir_lowering=False, num_devices=1)

    def plain(a):
        return np.ascontiguousarray(np.asarray(a))

    x, adj = plain(x), plain(adj)
    x_pad = np.zeros((NP, D), x.dtype)
    x_pad[:N] = x
    x_pad[N:] = x[N - 1:]
    adj_pad = np.zeros((NP, NP), adj.dtype)
    adj_pad[:N, :N] = adj
    adj_pad[N:, :N] = adj[N - 1:]

    def on_all(a):
        return plain(np.tile(plain(a).reshape(1, -1), (P, 1)))

    def by_feature(a):
        return plain(plain(a).reshape(-1, P).T)

    arrays = {
        "in_x": x_pad.reshape(NB, P, D),
        "in_adj": adj_pad,
        "in_eye": np.eye(P, dtype=np.float32),
        "in_w_sa": plain(L1_gnn_W_sa),
        "in_a_sa": on_all(L1_gnn_a_sa),
        "in_w_gcnb": plain(L1_gnn_W_gcnb),
        "in_b_gcnb": on_all(L1_gnn_b_gcnb),
        "in_gate_w": plain(np.stack([by_feature(L1_gnn_Wa), by_feature(L1_gnn_Wb)], axis=1)),
        "in_gate_b": plain(np.concatenate([on_all(L1_gnn_ba), on_all(L1_gnn_bb)], axis=1)),
        "in_w_q": plain(plain(L2_gnn_Wq).T),
        "in_w_k": plain(plain(L2_gnn_Wk).T),
        "in_w_v": plain(plain(L2_gnn_Wv).T),
        "in_b_q": by_feature(L2_gnn_bq),
        "in_b_k": by_feature(L2_gnn_bk),
        "in_b_v": on_all(L2_gnn_bv),
        "in_w_stack": plain(L3_gnn_W_stack),
    }
    args = [nc.dram_tensor(name, a.shape, mybir.dt.from_np(a.dtype), kind="ExternalInput").ap()
            for name, a in arrays.items()]
    out = nc.dram_tensor("out", (NB, P, D), F32, kind="ExternalOutput").ap()
    graph_layers(nc, *args, out)
    result = run_bass_kernel_spmd(nc, [arrays], core_ids=[0])
    return result.results[0]["out"].reshape(NP, D)[:N]
```

```python
from contextlib import ExitStack

import concourse.bass as bass
from concourse import mybir

P = 128
D = 256
DC = D // P
N = 3327
NB = -(-N // P)
NP = NB * P
CW = 512
NCH = -(-NP // CW)
GSTEPS = 2 * NCH
LN_EPS = 1e-5
SIGMOID_FROM = -87.0
LOW = -3.0e38

F32 = mybir.dt.float32
F32R = mybir.dt.float32r
ALU = mybir.AluOpType
ACT = mybir.ActivationFunctionType
AX = mybir.AxisListType

SCORES_AT = [(0, 1), (2, 3), (4,), (5,), (6,), (), ()]
MASKS_POOL = 4
COUNTS_AT = [(4,), (5, 0), (6, 1), (2, 3), (), (), ()]
assert [c for cs in SCORES_AT for c in cs] == list(range(NCH))


def width(c):
    return min(CW, NP - c * CW)


def live(c):
    return min(CW, N - c * CW)


def cols(c, w):
    return slice(c * CW, c * CW + w)


def wait_past(engine, semaphore, value):
    if isinstance(value, int) and value <= 0:
        return
    engine.wait_ge(semaphore, value)


def blocks(engine, slot):
    pairs = NB // 2
    for k in range(2):
        slot(0, k)
    with engine.Fori(1, pairs - 1) as half:
        for k in range(2):
            slot(half, k)
    for k in range(2):
        slot(pairs - 1, k)


def following(half, k):
    return (half, 1) if k == 0 else (half + 1, 0)


def previous(half, k):
    return (half, 0) if k == 1 else (half - 1, 1)


def chunk_after(half, k, c, steps=NCH, by=1):
    if c + by < steps:
        return half, k, c + by
    return None if is_last(half, k) else (*following(half, k), c + by - steps)


def lanes(period, ring):
    lane = [p % ring for p in range(period)]
    if lane[-1] == lane[0]:
        lane[-1] = (lane[-1] + 1) % ring
    ago = [next(a for a in range(1, period + 1) if lane[(p - a) % period] == lane[p]) for p in range(period)]
    assert min(ago) >= 2
    return lane, ago


AHEAD = 2
TURNS = {(NCH, 2): lanes(2 * NCH, 2), (NCH, 3): lanes(2 * NCH, 3), (GSTEPS, 3): lanes(2 * GSTEPS, 3)}


def stream(half, k, c, steps=NCH, ring=2):
    lane, ago = TURNS[steps, ring]
    return steps * (2 * half + k) + c, lane[steps * k + c], ago[steps * k + c]


def is_last(half, k):
    return isinstance(half, int) and 2 * half + k == NB - 1


def graph_layers(nc, x, adj, eye, w_sa, a_sa, w_gcnb, b_gcnb, gate_w, gate_b, w_q, w_k, w_v, b_q, b_k,
                 b_v, w_stack, out):
    with ExitStack() as ctx:
        def sb(name, shape, dt=F32):
            return ctx.enter_context(nc.sbuf_tensor(name, shape, dt))

        def sem(name):
            return ctx.enter_context(nc.semaphore(name))

        def sems(name):
            return [sem(f"{name}{k}") for k in range(2)]

        ps = ctx.enter_context(nc.psum_tensor("ps", [P, 8, CW], F32))
        score_ps = [ps[:, k, :] for k in range(2)]
        turn_ps = [ps[:, k, :] for k in (2, 3, 7)]
        sum_ps = [ps[:, 4 + k, :] for k in range(2)]
        small_ps = ps[:, 6, 0:D]
        mix_ps = ps[:, 6, :]

        def turned_h_ps(n):
            return ps[:, 6 if n < 2 else 7, 0:D]

        prep_a_ps = [ps[:, 6, 0:D], ps[:, 0, 0:D]]
        prep_b_ps = [ps[:, 7, :], ps[:, 1, :]]

        values = sb("values", [P, NB, 2, D], F32R)
        keys = sb("keys", [P, DC, 2, NP], F32R)
        values2 = keys[:].rearrange("p a b n -> p (a b n)").rearrange("p (j s d) -> p j s d", s=2, d=D)
        row_in = [sb(f"row_in{k}", [P, NP]) for k in range(2)]
        row = [sb(f"row{k}", [P, NP]) for k in range(2)]
        s_right = sb("s_right", [P, NP])
        s_left = sb("s_left", [P, NB, 2])
        queries = sb("queries", [P, 2, 2, DC, P], F32R)
        query_hi = [queries[:, 0, k] for k in range(2)]
        query_lo = [queries[:, 1, k] for k in range(2)]
        turned_hi = [sb(f"turned_hi{k}", [P, CW], F32R) for k in range(2)]
        turned_lo = [sb(f"turned_lo{k}", [P, CW], F32R) for k in range(2)]
        turned_hi.append(queries[:, 0].rearrange("p k c n -> p (k c n)"))
        turned_lo.append(queries[:, 1].rearrange("p k c n -> p (k c n)"))
        weights = sb("weights", [P, DC, 3 * D])
        ident = sb("ident", [P, P])
        ht_in = [sb(f"ht_in{k}", [P, DC, P]) for k in range(2)]
        base = [sb(f"base{k}", [P, D]) for k in range(2)]
        side = [sb(f"side{k}", [P, D]) for k in range(2)]
        side2 = [sb(f"side2{k}", [P, D]) for k in range(2)]
        new_x = [sb(f"new_x{k}", [P, D]) for k in range(2)]
        new_h = [sb(f"new_h{k}", [P, D]) for k in range(2)]
        new_ht = [sb(f"new_ht{k}", [P, DC, P]) for k in range(2)]
        stat = [sb(f"stat{k}", [P, 40]) for k in range(2)]
        part = [sb(f"part{k}", [P, 2, NCH]) for k in range(2)]
        spare = [sb(f"spare{k}", [P, NCH + 1]) for k in range(2)]
        norm_parts = sb("norm_parts", [P, NB, 6])
        norm = sb("norm", [P, NB, 4])
        minus_half = sb("minus_half", [P, NB // 2])
        plus_half = sb("plus_half", [P, 1])
        bias_row = sb("bias_row", [P, D])
        bias_col = sb("bias_col", [P, 2, DC])
        gate_cols = sb("gate_cols", [P, 2, 4])
        gate_bias = sb("gate_bias", [P, 2])
        fold = [sb(f"fold{k}", [P, DC, P]) for k in range(2)]

        sa_cols = weights[:, :, 0:D + 1]
        mix_cols = weights[:, :, D + 1:2 * D + 3]
        right_cols = weights[:, :, 2 * D + 3:2 * D + 3 + P]

        def dram(name, shape):
            return nc.dram_tensor(name, shape, F32, kind="Internal").ap()

        x_mid = [dram(f"x_mid{n}", (NB, P, D)) for n in range(4)]
        h_mid = [dram(f"h_mid{n}", (NB, P, D)) for n in range(3)]
        ht_mid = [dram(f"ht_mid{n}", (NB, P, DC, P)) for n in range(4)]
        adj_rows = adj.rearrange("(b p) n -> b p n", p=P)

        def st(k, a, w=1):
            return stat[k][:, a:a + w]

        consts_in = sem("consts_in")
        consts_set = sem("consts_set")
        out_stored = sems("out_stored")
        shared = {name: sem(name) for name in (
            "prep_hi", "prep_lo",
            "side_done", "sums_read")}
        shared.update({name: sems(name) for name in ("adj_in", "base_in", "ht_in")})
        frame = ["ready", "turned", "hi_done", "lo_done", "multiplied",
                 "chain2"]
        normed = ["var", "rstd"]
        features = ["h_done", "h_turned", "h_out"]
        attention = ["wts_in", "prep_mm", "query_mm", "query_hi", "query_lo",
                     "score_mm", "score_out", "top", "exp_done", "chain"]
        own_pairs = [["stored"], ["stored"], ["stored"], ["stored"], ["extra_in"]]
        own = [
            normed + features + ["prep_var", "prep_rstd", "prep_h", "prep_chain", "raw_done", "relu_done", "count_done",
                                 "inverse", "root", "chain"],
            normed + features + ["wts_in", "wts_set", "prep_mm", "prep_chain", "raw_done", "arg_done",
                                 "exp_done", "left_here", "ts_done", "ts_turned", "ts_out", "mix_mm", "gate_arg",
                                 "gate_exp", "sig_arg", "sig_tanh"],
            normed + features + attention + ["prep_fold", "query_fold"],
            features + attention,
            ["h_out"] + attention,
        ]
        phases = []
        for n in range(5):
            named = {name: sem(f"{name}_{n}") for name in frame + own[n]}
            named.update({name: sems(f"{name}_{n}_") for name in ["prep_in"] + own_pairs[n]})
            phases.append({**shared, **named, "layer": n, "block0": NB * n, "half0": NB // 2 * n,
                           "half1": NB // 2 * (n - 1)})

        block = ctx.enter_context(nc.Block())

        end = (NB // 2 - 1, 1)

        def alone(engine):
            engine.wait_ge(consts_in, 16)

        @block.sync
        def _(sp):
            sp.dma_start(ident[:], eye).then_inc(consts_in, 16)

            def at(array, b):
                if isinstance(b, int):
                    return array[b]
                view = array[bass.ds(b, 1)]
                names = " ".join("cde"[:len(array.shape) - 2])
                return view.rearrange(f"o p {names} -> (o p) {names}")

            def prep_loads(n, ht_from, h_from=None):
                s = phases[n]
                for k in range(2):
                    sp.dma_start(row_in[k][:], adj_rows[k]).then_inc(s["adj_in"][k], 16)

                def slot(half, k):
                    b = 2 * half + k
                    wait_past(sp, s["prep_mm"], b - 1)
                    sp.dma_start(ht_in[k][:], at(ht_from, b)).then_inc(s["prep_in"][k], 16)
                    if h_from is not None:
                        sp.dma_start(values[:, bass.ds(b, 1), 1, :].rearrange("p o d -> p (o d)").bitcast(F32),
                                     at(h_from, b)).then_inc(s["prep_in"][k], 16)

                blocks(sp, slot)

            def layer_loads(n, base_from, ht_from, stores, adj_freed, adj_per, extra_from=None):
                s = phases[n]

                def load_adj(half, k):
                    sp.wait_ge(adj_freed(s), adj_per * (2 * half + k - 1))
                    sp.dma_start(row_in[k][:], at(adj_rows, 2 * half + k)).then_inc(s["adj_in"][k], 16)

                def load_ht(half, k):
                    if n in (2, 3, 4):
                        wait_past(sp, s["query_mm"], 2 * half + k - 1)
                    else:
                        wait_past(sp, s["mix_mm"], 2 * half + k - 1)
                    sp.dma_start(ht_in[k][:], at(ht_from, 2 * half + k)).then_inc(s["ht_in"][k], 16)

                def store(half, k):
                    b = 2 * half + k
                    sp.wait_ge(s["h_out"], b + 1)
                    if n == 4:
                        sp.dma_start(at(out, b), new_x[k][:]).then_inc(out_stored[k], 16)
                        return
                    for tile, array in stores:
                        sp.dma_start(at(array, b), tile[k][:]).then_inc(s["stored"][k], 16)

                sp.wait_ge(s["prep_lo"], NB + s["block0"])
                for k in range(2):
                    if ht_from is not None:
                        load_ht(0, k)

                def slot(half, k):
                    b = 2 * half + k
                    wait_past(sp, s["h_out"], b - 1)
                    sp.dma_start(base[k][:], at(base_from, b)).then_inc(s["base_in"][k], 16)
                    if extra_from is not None:
                        sp.dma_start(side2[k][:], at(extra_from, b)).then_inc(s["extra_in"][k], 16)
                    if not (isinstance(half, int) and half == NB // 2 - 1):
                        if ht_from is not None:
                            load_ht(half + 1, k)
                        load_adj(half + 1, k)
                    if isinstance(half, int) and b == 0:
                        return
                    prev = (half, 0) if k == 1 else (half - 1, 1)
                    store(*prev)

                blocks(sp, slot)
                store(NB // 2 - 1, 1)
                if n < 4:
                    for k in range(2):
                        sp.wait_ge(s["stored"][k], 16 * len(stores) * (NB // 2))

            for k in range(2):
                for part_of in range(2):
                    sp.dma_start(row[k][:, part_of * 7 * D:(7 + part_of * 6) * D].rearrange("p (b d) -> p b d", d=D),
                                 x[k * NB // 2 + part_of * 7:k * NB // 2 + 7 + part_of * 6].rearrange("b p d -> p b d"))\
                      .then_inc(phases[0]["prep_in"][k], 16)
            for k in range(2):
                sp.dma_start(row_in[k][:], adj_rows[k]).then_inc(phases[0]["adj_in"][k], 16)
            layer_loads(0, x, None, [(new_x, x_mid[0]), (new_h, h_mid[0]), (new_ht, ht_mid[0])],
                        lambda s: s["ready"], NCH)

            s = phases[1]
            rows_of = "(c p) n -> p c n"
            sp.dma_start(weights[:, :, 0:D], w_sa.rearrange(rows_of, p=P)).then_inc(s["wts_in"], 16)
            sp.dma_start(weights[:, :, D + 1:2 * D + 1], w_gcnb.rearrange(rows_of, p=P)).then_inc(s["wts_in"], 16)
            sp.dma_start(side[0][:], a_sa[:, 0:D]).then_inc(s["wts_in"], 16)
            sp.dma_start(side[1][:], a_sa[:, D:2 * D]).then_inc(s["wts_in"], 16)
            sp.dma_start(bias_row[:], b_gcnb).then_inc(s["wts_in"], 16)
            sp.dma_start(gate_cols[:], gate_w).then_inc(s["wts_in"], 16)
            sp.dma_start(gate_bias[:], gate_b).then_inc(s["wts_in"], 16)
            prep_loads(1, ht_mid[0], h_mid[0])
            layer_loads(1, x_mid[0], ht_mid[0], [(new_x, x_mid[1]), (new_ht, ht_mid[1])],
                        lambda s: s["turned"], GSTEPS)

            s = phases[2]
            for i, w in enumerate((w_q, w_k, w_v)):
                sp.dma_start(weights[:, :, i * D:(i + 1) * D], w.rearrange(rows_of, p=P)).then_inc(s["wts_in"], 16)
            sp.dma_start(bias_row[:], b_v).then_inc(s["wts_in"], 16)
            sp.dma_start(bias_col[:, 0, :], b_q).then_inc(s["wts_in"], 16)
            sp.dma_start(bias_col[:, 1, :], b_k).then_inc(s["wts_in"], 16)
            prep_loads(2, ht_mid[1])
            layer_loads(2, x_mid[1], ht_mid[1], [(new_x, x_mid[2]), (new_h, h_mid[1]), (new_ht, ht_mid[2])],
                        lambda s: s["score_out"], NCH)

            for n in (3, 4):
                s = phases[n]
                w = w_stack[n - 3].rearrange(rows_of, p=P)
                sp.dma_start(weights[:, :, 0:2 * D], w).then_inc(s["wts_in"], 16)
                prep_loads(n, ht_mid[n - 1])
                if n == 3:
                    layer_loads(3, h_mid[1], ht_mid[2], [(new_x, h_mid[2]), (new_ht, ht_mid[3])],
                                lambda s: s["ready"], NCH)
                else:
                    layer_loads(4, h_mid[2], ht_mid[3], [], lambda s: s["ready"], NCH, extra_from=x_mid[2])
            for k in range(2):
                sp.wait_ge(out_stored[k], 16 * (NB // 2))

        @block.tensor
        def _(pe):
            pe.wait_ge(consts_in, 16)

            def turn(s, src, g, c, source_ready):
                value, j, ago = g
                wait_past(pe, s["lo_done"], value - ago + 1)
                source_ready()
                for i in range(width(c) // P):
                    mm = pe.transpose(turn_ps[j][:, i * P:(i + 1) * P], src[:, c * CW + i * P:c * CW + (i + 1) * P],
                                      ident[:])
                mm.then_inc(s["turned"], 1)

            def multiply(s, bank, vals, g, c):
                value, j, _ = g
                pe.wait_ge(s["lo_done"], value + 1)
                for i in range(width(c) // P):
                    jb = c * (CW // P) + i
                    pe.matmul(bank, turned_hi[j][:, i * P:(i + 1) * P],
                              vals[:, jb, :, :].rearrange("p s d -> p (s d)"),
                              start=(jb == 0), stop=False, skip_group_check=True)
                    mm = pe.matmul(bank[:, 0:D], turned_lo[j][:, i * P:(i + 1) * P], vals[:, jb, 0, :],
                                   start=False, stop=(jb == NB - 1), skip_group_check=True)
                mm.then_inc(s["multiplied"], 1)

            def turn_h(s, half, k):
                pe.wait_ge(s["h_done"], 2 * half + k + 1)
                src = new_x[k] if s["layer"] == 3 else new_h[k]
                for i in range(DC):
                    mm = pe.transpose(turned_h_ps(s["layer"])[:, i * P:(i + 1) * P], src[:, i * P:(i + 1) * P], ident[:])
                mm.then_inc(s["h_turned"], 1)

            s = phases[0]
            pe.wait_ge(s["prep_lo"], NB + s["block0"])

            def turn_row(s, half, k, c, ring=2):
                turn(s, row[k], stream(half, k, c, ring=ring), c,
                     lambda: pe.wait_ge(s["ready"], NCH * (2 * half + k) + c + 1))

            def layer0(half, k):
                b = 2 * half + k
                wait_past(pe, s["sums_read"], b - 1 + s["block0"])
                for c in range(NCH):
                    if after := chunk_after(half, k, c, by=AHEAD):
                        turn_row(s, *after, ring=3)
                    multiply(s, sum_ps[k], values, stream(half, k, c, ring=3), c)
                    if c == 4 and not (isinstance(half, int) and b == 0):
                        turn_h(s, *previous(half, k))

            for c in range(AHEAD):
                turn_row(s, 0, 0, c, ring=3)
            blocks(pe, layer0)
            turn_h(s, NB // 2 - 1, 1)

            s = phases[1]
            pe.wait_ge(s["wts_set"], 1)

            def prep1(half, k):
                b = 2 * half + k
                pe.wait_ge(s["prep_in"][k], 32 * (half + 1))
                wait_past(pe, s["prep_lo"], b - 1 + s["block0"])
                for i in range(DC):
                    pe.matmul(prep_b_ps[k][:, 0:D + 1], ht_in[k][:, i, :], sa_cols[:, i, :], start=(i == 0),
                              stop=(i == DC - 1))
                for i in range(DC):
                    mm = pe.matmul(prep_a_ps[k][:, 0:P], right_cols[:, i, :], ht_in[k][:, i, :],
                                   start=(i == 0), stop=(i == DC - 1))
                mm.then_inc(s["prep_mm"], 1)

            blocks(pe, prep1)
            pe.wait_ge(s["prep_lo"], NB + s["block0"])

            def turn_step(half, k, g):
                if g < NCH:
                    turn(s, row_in[k], stream(half, k, g, GSTEPS, 3), g,
                         lambda: pe.wait_ge(s["adj_in"][k], 16 * (half + 1 + s["half0"])))
                else:
                    turn(s, row[k], stream(half, k, g, GSTEPS, 3), g - NCH,
                         lambda: pe.wait_ge(s["ready"], NCH * (2 * half + k) + g - NCH + 1))

            def layer1(half, k):
                b = 2 * half + k
                wait_past(pe, s["sums_read"], b - 1 + s["block0"])
                for g in range(GSTEPS):
                    if after := chunk_after(half, k, g, GSTEPS, AHEAD):
                        turn_step(*after)
                    if g < NCH:
                        multiply(s, sum_ps[k], values, stream(half, k, g, GSTEPS, 3), g)
                    else:
                        multiply(s, score_ps[k], values2, stream(half, k, g, GSTEPS, 3), g - NCH)
                    if not (isinstance(half, int) and b == 0):
                        if g == 3:
                            turn_ts(*previous(half, k))
                        if g == 5:
                            mix(*previous(half, k))
                        if g == 13:
                            turn_h(s, *previous(half, k))

            def turn_ts(half, k):
                wait_past(pe, s["h_out"], 2 * half + k)
                pe.wait_ge(s["ts_done"], 2 * half + k + 1)
                for i in range(DC):
                    mm = pe.transpose(small_ps[:, i * P:(i + 1) * P], side2[k][:, i * P:(i + 1) * P], ident[:])
                mm.then_inc(s["ts_turned"], 1)

            def mix(half, k):
                pe.wait_ge(s["ts_out"], 2 * half + k + 1)
                pe.wait_ge(s["ht_in"][k], 16 * (half + 1 + s["half1"]))
                for i in range(DC):
                    pe.matmul(mix_ps[:, 0:D + 2], fold[k][:, i, :], mix_cols[:, i, :], start=(i == 0), stop=False,
                              skip_group_check=True)
                for i in range(DC):
                    mm = pe.matmul(mix_ps[:, D:D + 2], ht_in[k][:, i, :], gate_cols[:, :, 2 + i], start=False,
                                   stop=(i == DC - 1), skip_group_check=True)
                mm.then_inc(s["mix_mm"], 1)

            for g in range(AHEAD):
                turn_step(0, 0, g)
            blocks(pe, layer1)
            turn_ts(NB // 2 - 1, 1)
            mix(NB // 2 - 1, 1)
            turn_h(s, NB // 2 - 1, 1)

            for n in (2, 3, 4):
                s = phases[n]
                key_at = D
                value_at = 2 * D if n == 2 else 0
                pe.wait_ge(s["wts_in"], 16 * (6 if n == 2 else 1))

                def prep(half, k):
                    b = 2 * half + k
                    pe.wait_ge(s["prep_in"][k], 16 * (half + 1))
                    wait_past(pe, s["prep_lo"], b - 1 + s["block0"])
                    for o in range(DC):
                        for i in range(DC):
                            pe.matmul(prep_a_ps[k][:, o * P:(o + 1) * P],
                                      weights[:, i, key_at + o * P:key_at + (o + 1) * P], ht_in[k][:, i, :],
                                      start=(i == 0), stop=(i == DC - 1))
                    for i in range(DC):
                        mm = pe.matmul(prep_b_ps[k][:, 0:D], ht_in[k][:, i, :],
                                       weights[:, i, value_at:value_at + D], start=(i == 0), stop=(i == DC - 1))
                    mm.then_inc(s["prep_mm"], 1)

                blocks(pe, prep)
                pe.wait_ge(s["prep_lo"], NB + s["block0"])

                def query(half, k):
                    b = 2 * half + k
                    pe.wait_ge(s["ht_in"][k], 16 * (half + 1 + s["half1"]))
                    wait_past(pe, s["query_lo"], b)
                    for o in range(DC):
                        for i in range(DC):
                            mm = pe.matmul(small_ps[:, o * P:(o + 1) * P], weights[:, i, o * P:(o + 1) * P],
                                           ht_in[k][:, i, :], start=(i == 0), stop=(i == DC - 1))
                    mm.then_inc(s["query_mm"], 1)

                def scores(half, k, c):
                    b = 2 * half + k
                    j = (NCH * k + c) % 2
                    pe.wait_ge(s["query_lo"], b + 1)
                    wait_past(pe, s["score_out"], NCH * b + c - 1)
                    w = width(c)
                    for i in range(DC):
                        for q, side_of_key in ((query_hi, 0), (query_hi, 1), (query_lo, 0)):
                            mm = pe.matmul(score_ps[j][:, 0:w], q[k][:, i, :], keys[:, i, side_of_key, cols(c, w)],
                                           start=(i == 0 and q is query_hi and side_of_key == 0),
                                           stop=(i == DC - 1 and q is query_lo))
                    mm.then_inc(s["score_mm"], 1)

                query(0, 0)
                query(0, 1)
                for c in range(NCH):
                    scores(0, 0, c)

                turn_row(s, 0, 0, 0)

                def attend(half, k):
                    b = 2 * half + k
                    wait_past(pe, s["sums_read"], b - 1 + s["block0"])
                    for c in range(NCH):
                        if not is_last(half, k):
                            for a in SCORES_AT[c]:
                                scores(*following(half, k), a)
                        if after := chunk_after(half, k, c):
                            turn_row(s, *after)
                        multiply(s, sum_ps[k], values, stream(half, k, c), c)
                        if c == 4 and not (isinstance(half, int) and b == 0) and n < 4:
                            turn_h(s, *previous(half, k))
                        if c == 5 and not (isinstance(half, int) and half == NB // 2 - 1):
                            query(half + 1, k)

                blocks(pe, attend)
                if n < 4:
                    turn_h(s, NB // 2 - 1, 1)

        @block.scalar
        def _(act):
            def hi_part(s, g, c):
                value, j, ago = g
                act.wait_ge(s["turned"], value + 1)
                wait_past(act, s["multiplied"], value - ago + 1)
                act.activation(turned_hi[j][:, 0:width(c)], turn_ps[j][:, 0:width(c)], ACT.Copy)\
                   .then_inc(s["hi_done"], 1)

            def side_copy(s, half, k):
                b = 2 * half + k
                steps = GSTEPS if s["layer"] == 1 else NCH
                act.wait_ge(s["multiplied"], steps * (b + 1))
                wait_past(act, s["sums_read"], b - 1 + s["block0"])
                if s["layer"] == 1:
                    act.activation(new_h[k][:], score_ps[k][:, D:2 * D], ACT.Copy)
                act.activation(side[k][:], sum_ps[k][:, D:2 * D], ACT.Copy).then_inc(s["side_done"], 1)

            def ht_copy(s, half, k):
                b = 2 * half + k
                act.wait_ge(s["h_turned"], b + 1)
                stores = {0: 3, 1: 2, 2: 3, 3: 2}[s["layer"]]
                wait_past(act, s["stored"][k], 16 * stores * half)
                act.activation(new_ht[k][:].rearrange("p c n -> p (c n)"), turned_h_ps(s["layer"]), ACT.Copy)\
                   .then_inc(s["h_out"], 1)

            s = phases[0]

            half_nb = NB // 2
            for k in range(2):
                act.wait_ge(s["prep_h"], k + 1)
                act.activation(values[:, k * half_nb:(k + 1) * half_nb, 0, :],
                               row[k][:].rearrange("p (b d) -> p b d", d=D), ACT.Relu).then_inc(s["prep_hi"], half_nb)

            def count(half, k, c):
                b = 2 * half + k
                tile = row[k][:, cols(c, width(c))]
                if c < MASKS_POOL:
                    act.wait_ge(s["raw_done"], MASKS_POOL * b + c + 1)
                    act.activation(tile, tile, ACT.Copy, accum_out=part[k][:, 0, c:c + 1])\
                       .then_inc(s["count_done"], 1)
                    return
                act.wait_ge(s["adj_in"][k], 16 * (half + 1 + s["half0"]))
                wait_past(act, s["turned"], NCH * (b - 1))
                act.activation(tile, row_in[k][:, cols(c, width(c))], ACT.Relu).then_inc(s["relu_done"], 1)
                act.wait_ge(s["relu_done"], (NCH - MASKS_POOL) * b + c - MASKS_POOL + 1)
                act.activation(tile, tile, ACT.Sign, accum_out=part[k][:, 0, c:c + 1])\
                   .then_inc(s["count_done"], 1)

            act.wait_ge(s["prep_lo"], NB)
            for a in [c for cs in COUNTS_AT for c in cs]:
                count(0, 0, a)

            def layer0(half, k):
                b = 2 * half + k
                for c in range(NCH):
                    if after := chunk_after(half, k, c, by=AHEAD):
                        hi_part(s, stream(*after, ring=3), after[2])
                    if not is_last(half, k):
                        for a in COUNTS_AT[c]:
                            count(*following(half, k), a)
                    if not (isinstance(half, int) and b == 0):
                        if c == 0:
                            side_copy(s, *previous(half, k))
                        if c == 5:
                            ht_copy(s, *previous(half, k))

            for c in range(AHEAD):
                hi_part(s, stream(0, 0, c, ring=3), c)
            blocks(act, layer0)
            side_copy(s, NB // 2 - 1, 1)
            ht_copy(s, NB // 2 - 1, 1)

            s = phases[1]

            def prep1(half, k):
                b = 2 * half + k
                act.wait_ge(s["prep_in"][k], 32 * (half + 1))
                alone(act)
                act.activation(values[:, bass.ds(b, 1), 0, :].rearrange("p o d -> p (o d)"),
                               values[:, bass.ds(b, 1), 1, :].rearrange("p o d -> p (o d)").bitcast(F32), ACT.Copy)
                act.wait_ge(s["prep_mm"], b + 1)
                alone(act)
                act.activation(s_right[:, bass.ds(b * P, P)], prep_a_ps[k][:, 0:P], ACT.Copy)
                act.activation(values2[:, bass.ds(b, 1), 0, :].rearrange("p o d -> p (o d)"),
                               prep_b_ps[k][:, 0:D], ACT.Copy).then_inc(s["prep_hi"], 1)

            blocks(act, prep1)
            act.wait_ge(s["prep_lo"], NB + s["block0"])

            def positive_part(half, k, c):
                b = 2 * half + k
                if c == 0:
                    act.wait_ge(s["left_here"], b + 1)
                wait_past(act, s["turned"], GSTEPS * (b - 2) + NCH + c + 1)
                act.activation(row[k][:, cols(c, width(c))], s_right[:, cols(c, width(c))], ACT.Relu,
                               bias=st(k, 26), scale=99.0).then_inc(s["raw_done"], 1)

            def exponential(half, k, c):
                b = 2 * half + k
                act.wait_ge(s["arg_done"], NCH * b + c + 1)
                act.activation(row[k][:, cols(c, width(c))], row[k][:, cols(c, width(c))], ACT.Exp,
                               bias=st(k, 27), scale=-0.01).then_inc(s["exp_done"], 1)

            for c in range(NCH):
                positive_part(0, 0, c)
            for c in range(NCH):
                exponential(0, 0, c)

            def ts_copy(half, k):
                act.wait_ge(s["ts_turned"], 2 * half + k + 1)
                act.activation(fold[k][:].rearrange("p c n -> p (c n)"), small_ps, ACT.Copy).then_inc(s["ts_out"], 1)

            def gate_exp(half, k):
                act.wait_ge(s["gate_arg"], 2 * half + k + 1)
                act.activation(st(k, 2, 2), st(k, 0, 2), ACT.Exp, scale=-1.0).then_inc(s["gate_exp"], 1)

            def sig_tanh(half, k):
                act.wait_ge(s["sig_arg"], 2 * half + k + 1)
                act.activation(side[k][:], side2[k][:], ACT.Tanh, scale=0.5).then_inc(s["sig_tanh"], 1)

            def layer1(half, k):
                b = 2 * half + k
                for g in range(GSTEPS):
                    if after := chunk_after(half, k, g, GSTEPS, AHEAD):
                        hi_part(s, stream(*after, GSTEPS, 3), after[2] % NCH)
                    if not is_last(half, k):
                        if g < NCH:
                            positive_part(*following(half, k), g)
                        else:
                            exponential(*following(half, k), g - NCH)
                    if not (isinstance(half, int) and b == 0):
                        prev = previous(half, k)
                        if g == 0:
                            side_copy(s, *prev)
                        if g == 3:
                            ts_copy(*prev)
                        if g == 6:
                            gate_exp(*prev)
                        if g == 9:
                            sig_tanh(*prev)
                        if g == 13:
                            ht_copy(s, *prev)

            for g in range(AHEAD):
                hi_part(s, stream(0, 0, g, GSTEPS, 3), g)
            blocks(act, layer1)
            side_copy(s, *end)
            ts_copy(*end)
            gate_exp(*end)
            sig_tanh(*end)
            ht_copy(s, *end)

            for n in (2, 3, 4):
                s = phases[n]

                def prep(half, k):
                    b = 2 * half + k
                    if n == 2:
                        act.wait_ge(s["prep_fold"], b + 1)
                        key_src = fold[k][:]
                        value_src = new_h[k][:]
                    else:
                        act.wait_ge(s["prep_mm"], b + 1)
                        key_src = prep_a_ps[k].rearrange("p (c n) -> p c n", c=DC)
                        value_src = prep_b_ps[k][:, 0:D]
                    alone(act)
                    act.activation(keys[:, :, 0, bass.ds(b * P, P)], key_src, ACT.Copy)
                    act.activation(values[:, bass.ds(b, 1), 0, :].rearrange("p o d -> p (o d)"), value_src,
                                   ACT.Copy).then_inc(s["prep_hi"], 1)

                blocks(act, prep)

                def query_hi_part(half, k):
                    b = 2 * half + k
                    wait_past(act, s["score_mm"], NCH * (b - 1))
                    if n == 2:
                        act.wait_ge(s["query_fold"], b + 1)
                        act.activation(query_hi[k], fold[k][:], ACT.Copy, scale=1.0 / 32)\
                           .then_inc(s["query_hi"], 1)
                    else:
                        act.wait_ge(s["query_mm"], b + 1)
                        act.activation(query_hi[k], small_ps.rearrange("p (c n) -> p c n", c=DC), ACT.Copy)\
                           .then_inc(s["query_hi"], 1)

                query_hi_part(0, 0)
                query_hi_part(0, 1)

                def exponential(half, k, c):
                    b = 2 * half + k
                    if c == 0:
                        act.wait_ge(s["top"], b + 1)
                    act.activation(row[k][:, cols(c, live(c))], row[k][:, cols(c, live(c))], ACT.Exp,
                                   bias=st(k, 1), accum_out=part[k][:, 1, c:c + 1])\
                       .then_inc(s["ready"] if n == 2 else s["exp_done"], 1)

                def attend(half, k):
                    b = 2 * half + k
                    for c in range(NCH):
                        if c + 2 < NCH:
                            exponential(half, k, c + 2)
                        elif not is_last(half, k):
                            exponential(*following(half, k), c + 2 - NCH)
                        if after := chunk_after(half, k, c):
                            hi_part(s, stream(*after), after[2])
                        if not (isinstance(half, int) and b == 0):
                            if c == 0:
                                side_copy(s, *previous(half, k))
                            if c == 4 and n < 4:
                                ht_copy(s, *previous(half, k))
                        if c == 5 and not (isinstance(half, int) and half == NB // 2 - 1):
                            query_hi_part(half + 1, k)

                exponential(0, 0, 0)
                exponential(0, 0, 1)
                hi_part(s, stream(0, 0, 0), 0)
                blocks(act, attend)
                side_copy(s, *end)
                if n < 4:
                    ht_copy(s, *end)

        @block.vector
        def _(dve):
            nc.vector.memset(minus_half[:], -0.5).then_inc(consts_set, 1)
            nc.vector.memset(plus_half[:], 0.5).then_inc(consts_set, 1)

            def chained(semaphore, before):
                done = [0]

                def link(instruction):
                    done[0] += 1
                    instruction.then_inc(semaphore, 1)
                    dve.wait_ge(semaphore, before + done[0])

                return link

            def lo_part(s, g, c):
                value, j, ago = g
                dve.wait_ge(s["hi_done"], value + 1)
                wait_past(dve, s["multiplied"], value - ago + 1)
                dve.tensor_tensor(turned_lo[j][:, 0:width(c)], turn_ps[j][:, 0:width(c)],
                                  turned_hi[j][:, 0:width(c)].bitcast(F32), ALU.subtract).then_inc(s["lo_done"], 1)

            def take_wait(k, column):
                dve.memset(spare[k][:, column:column + 1], 0.0)

            def variance(link, src, k, semaphore):
                link(dve.bn_stats(st(k, 4, 6), src))
                take_wait(k, NCH)
                link(dve.bn_aggr(st(k, 10, 2), st(k, 4, 6)))
                dve.tensor_scalar(st(k, 12), st(k, 11), LN_EPS, None, ALU.add).then_inc(semaphore, 1)

            def relu_norm(link, src, k, rstd_ready, semaphore):
                rstd_ready()
                link(dve.tensor_scalar(new_h[k][:], src, st(k, 10), st(k, 13), ALU.subtract, ALU.mult))
                dve.tensor_scalar(new_h[k][:], new_h[k][:], 0.0, None, ALU.max).then_inc(semaphore, 1)

            s = phases[0]

            half_nb = NB // 2
            link = chained(s["prep_chain"], 0)
            for k in range(2):
                dve.wait_ge(s["prep_in"][k], 32)
                for j in range(half_nb):
                    last = dve.bn_stats(norm_parts[:, k * half_nb + j, :], row[k][:, j * D:(j + 1) * D])
                link(last)
                for j in range(half_nb):
                    last = dve.bn_aggr(norm[:, k * half_nb + j, 0:2], norm_parts[:, k * half_nb + j, :])
                link(last)
                of_k = slice(k * half_nb, (k + 1) * half_nb)
                dve.tensor_scalar(norm[:, of_k, 2], norm[:, of_k, 1], LN_EPS, None, ALU.add).then_inc(s["prep_var"], 1)
            for k in range(2):
                dve.wait_ge(s["prep_rstd"], k + 1)
                for j in range(half_nb):
                    b = k * half_nb + j
                    last = dve.tensor_scalar(row[k][:, j * D:(j + 1) * D], row[k][:, j * D:(j + 1) * D],
                                             norm[:, b, 0:1], norm[:, b, 3:4], ALU.subtract, ALU.mult)
                last.then_inc(s["prep_h"], 1)
            for k in range(2):
                dve.wait_ge(s["prep_hi"], (k + 1) * half_nb)
                of_k = slice(k * half_nb, (k + 1) * half_nb)
                dve.scalar_tensor_tensor(out=values[:, of_k, 1, :], in0=row[k][:].rearrange("p (b d) -> p b d", d=D),
                                         scalar=0.0, in1=values[:, of_k, 0, :].bitcast(F32), op0=ALU.max,
                                         op1=ALU.subtract).then_inc(s["prep_lo"], half_nb)

            def degree_count(half, k):
                b = 2 * half + k
                dve.wait_ge(s["count_done"], NCH * (b + 1))
                dve.tensor_reduce(st(k, 14), part[k][:, 0, :], AX.X, ALU.add).then_inc(s["inverse"], 1)

            def inverse_norm(half, k):
                b = 2 * half + k
                link = chained(s["chain"], 2 * b)
                dve.wait_ge(s["root"], b + 1)
                link(dve.tensor_scalar(st(k, 16), st(k, 15), 1e-12, None, ALU.max))
                link(dve.reciprocal(st(k, 16), st(k, 16)))

            def incidence(half, k, c):
                w = width(c)
                dve.scalar_tensor_tensor(out=row[k][:, cols(c, w)], in0=row[k][:, cols(c, w)], scalar=st(k, 16),
                                         in1=row_in[k][:, cols(c, w)], op0=ALU.mult, op1=ALU.add,
                                         accum_out=part[k][:, 1, c:c + 1]).then_inc(s["ready"], 1)

            def epilogue0(half, k):
                b = 2 * half + k
                link = chained(s["chain2"], 6 * b)
                link(dve.tensor_reduce(st(k, 17), part[k][:, 1, :], AX.X, ALU.add))
                link(dve.reciprocal(st(k, 18), st(k, 17)))
                dve.wait_ge(s["side_done"], b + 1 + s["block0"])
                dve.wait_ge(s["base_in"][k], 16 * (half + 1 + s["half0"]))
                wait_stores(s, 3, half, k)
                dve.tensor_tensor(new_x[k][:], sum_ps[k][:, 0:D], side[k][:], ALU.add).then_inc(s["sums_read"], 1)
                dve.wait_ge(s["sums_read"], b + 1 + s["block0"])
                link(dve.scalar_tensor_tensor(out=new_x[k][:], in0=new_x[k][:], scalar=st(k, 18), in1=base[k][:],
                                              op0=ALU.mult, op1=ALU.add))
                variance(link, new_x[k][:], k, s["var"])

            def wait_stores(s, stores, half, k):
                wait_past(dve, s["stored"][k], 16 * stores * half)

            def epilogue_h(s, half, k, per):
                b = 2 * half + k
                link = chained(s["chain2"], per * b + per - 1)
                relu_norm(link, new_x[k][:], k, lambda: dve.wait_ge(s["rstd"], b + 1), s["h_done"])

            def layer0(half, k):
                b = 2 * half + k
                for c in range(NCH):
                    if after := chunk_after(half, k, c, by=AHEAD + 1):
                        if after[2] == 0:
                            inverse_norm(*after[:2])
                        incidence(*after)
                    if after := chunk_after(half, k, c, by=AHEAD):
                        lo_part(s, stream(*after, ring=3), after[2])
                    if c == 3 and not is_last(half, k):
                        degree_count(*following(half, k))
                    if not (isinstance(half, int) and b == 0):
                        if c == 1:
                            epilogue0(*previous(half, k))
                        if c == 3:
                            epilogue_h(s, *previous(half, k), 6)

            degree_count(0, 0)
            inverse_norm(0, 0)
            for c in range(AHEAD + 1):
                incidence(0, 0, c)
            for c in range(AHEAD):
                lo_part(s, stream(0, 0, c, ring=3), c)
            blocks(dve, layer0)
            epilogue0(*end)
            epilogue_h(s, *end, 6)

            s = phases[1]
            dve.wait_ge(s["wts_in"], 7 * 16)
            link = chained(s["prep_chain"], 0)
            for i in range(DC):
                link(dve.tensor_tensor_reduce(row[1][:, 0:D], weights[:, i, 0:D], side[0][:], 1.0, 0.0, ALU.mult,
                                              ALU.add, sa_cols[:, i, D:D + 1]))
                link(dve.tensor_tensor_reduce(row[1][:, 0:D], weights[:, i, 0:D], side[1][:], 1.0, 0.0, ALU.mult,
                                              ALU.add, st(0, 20 + i)))
            link(dve.memset(row[1][:, 0:P], 1.0))
            for i in range(DC):
                link(dve.tensor_scalar(right_cols[:, i, :], row[1][:, 0:P], st(0, 20 + i), None, ALU.mult))
            dve.tensor_copy(mix_cols[:, :, D:D + 2], gate_cols[:, :, 0:DC].rearrange("p g c -> p c g"))\
               .then_inc(s["wts_set"], 1)

            def prep1(half, k):
                b = 2 * half + k
                dve.wait_ge(s["prep_hi"], b + 1 + s["block0"])
                dve.tensor_scalar(s_left[:, bass.ds(b, 1), 0], prep_b_ps[k][:, D:D + 1], 99.0, None, ALU.mult)
                dve.tensor_scalar(s_left[:, bass.ds(b, 1), 1], prep_b_ps[k][:, D:D + 1], -0.01, None, ALU.mult)
                dve.tensor_tensor(values[:, bass.ds(b, 1), 1, :].rearrange("p o d -> p (o d)"),
                                  values[:, bass.ds(b, 1), 1, :].rearrange("p o d -> p (o d)").bitcast(F32),
                                  values[:, bass.ds(b, 1), 0, :].rearrange("p o d -> p (o d)").bitcast(F32),
                                  ALU.subtract)
                dve.tensor_tensor(values2[:, bass.ds(b, 1), 1, :].rearrange("p o d -> p (o d)"),
                                  prep_b_ps[k][:, 0:D],
                                  values2[:, bass.ds(b, 1), 0, :].rearrange("p o d -> p (o d)").bitcast(F32),
                                  ALU.subtract).then_inc(s["prep_lo"], 1)

            blocks(dve, prep1)

            def masked(half, k, c):
                b = 2 * half + k
                w = width(c)
                dve.wait_ge(s["adj_in"][k], 16 * (half + 1 + s["half0"]))
                dve.wait_ge(s["exp_done"], NCH * b + c + 1)
                dve.scalar_tensor_tensor(out=row[k][:, cols(c, w)], in0=row_in[k][:, cols(c, w)], scalar=0.0,
                                         in1=row[k][:, cols(c, w)], op0=ALU.not_equal, op1=ALU.mult,
                                         accum_out=part[k][:, 0, c:c + 1]).then_inc(s["ready"], 1)

            def left(half, k):
                dve.tensor_scalar(st(k, 26, 2), s_left[:, bass.ds(2 * half + k, 1), :]
                                  .rearrange("p o t -> p (o t)"), 1.0, None, ALU.mult).then_inc(s["left_here"], 1)

            dve.wait_ge(s["prep_lo"], NB + s["block0"])
            left(0, 0)
            for c in range(NCH):
                masked(0, 0, c)
            for g in range(AHEAD):
                lo_part(s, stream(0, 0, g, GSTEPS, 3), g)

            PER1 = 14

            def sums1(half, k):
                b = 2 * half + k
                link = chained(s["chain2"], PER1 * b)
                dve.wait_ge(s["side_done"], b + 1 + s["block0"])
                dve.tensor_tensor(side2[k][:], sum_ps[k][:, 0:D], side[k][:], ALU.add).then_inc(s["ts_done"], 1)
                wait_stores(s, 2, half, k)
                dve.tensor_tensor(new_x[k][:], score_ps[k][:, 0:D], new_h[k][:], ALU.add).then_inc(s["sums_read"], 1)
                link(dve.tensor_reduce(st(k, 14), part[k][:, 0, :], AX.X, ALU.add))
                link(dve.tensor_scalar(st(k, 15), st(k, 14), 1e-5, None, ALU.add))
                link(dve.reciprocal(st(k, 16), st(k, 15)))

            def gates1(half, k):
                b = 2 * half + k
                dve.wait_ge(s["mix_mm"], b + 1)
                link = chained(s["chain2"], PER1 * b + 3)
                link(dve.tensor_tensor(st(k, 0, 2), mix_ps[:, D:D + 2], gate_bias[:], ALU.add))
                dve.tensor_scalar(st(k, 0, 2), st(k, 0, 2), SIGMOID_FROM, None, ALU.max).then_inc(s["gate_arg"], 1)
                link(dve.tensor_tensor(side2[k][:], mix_ps[:, 0:D], bias_row[:], ALU.add))

            def mixed1(half, k):
                b = 2 * half + k
                link = chained(s["chain2"], PER1 * b + 5)
                dve.wait_ge(s["gate_exp"], b + 1)
                link(dve.tensor_scalar(st(k, 20, 2), st(k, 2, 2), 1.0, None, ALU.add))
                link(dve.reciprocal(st(k, 22, 2), st(k, 20, 2)))
                link(dve.tensor_tensor(st(k, 24), st(k, 22), st(k, 16), ALU.mult))
                link(dve.tensor_scalar(side2[k][:], side2[k][:], st(k, 23), None, ALU.mult))
                dve.scalar_tensor_tensor(out=side2[k][:], in0=new_x[k][:], scalar=st(k, 24), in1=side2[k][:],
                                         op0=ALU.mult, op1=ALU.add).then_inc(s["sig_arg"], 1)

            def result1(half, k):
                b = 2 * half + k
                link = chained(s["chain2"], PER1 * b + 9)
                dve.wait_ge(s["sig_tanh"], b + 1)
                dve.wait_ge(s["base_in"][k], 16 * (half + 1 + s["half0"]))
                link(dve.tensor_scalar(new_x[k][:], side[k][:], 0.5, 0.5, ALU.mult, ALU.add))
                link(dve.tensor_tensor(new_x[k][:], new_x[k][:], base[k][:], ALU.add))
                variance(link, new_x[k][:], k, s["var"])

            def layer1(half, k):
                b = 2 * half + k
                if not is_last(half, k):
                    left(*following(half, k))
                for g in range(GSTEPS):
                    if g > NCH and not is_last(half, k):
                        masked(*following(half, k), g - NCH - 1)
                    if g == GSTEPS - 1 and not is_last(half, k):
                        masked(*following(half, k), NCH - 1)
                    if after := chunk_after(half, k, g, GSTEPS, AHEAD):
                        lo_part(s, stream(*after, GSTEPS, 3), after[2] % NCH)
                    if not (isinstance(half, int) and b == 0):
                        prev = previous(half, k)
                        if g == 1:
                            sums1(*prev)
                        if g == 6:
                            gates1(*prev)
                        if g == 7:
                            mixed1(*prev)
                        if g == 10:
                            result1(*prev)
                        if g == 12:
                            epilogue_h(s, *prev, PER1)

            blocks(dve, layer1)
            sums1(*end)
            gates1(*end)
            mixed1(*end)
            result1(*end)
            epilogue_h(s, *end, PER1)

            for n in (2, 3, 4):
                s = phases[n]
                if n == 2:
                    dve.wait_ge(s["wts_in"], 6 * 16)
                    for k in range(2):
                        dve.memset(row[k][:, N:NP], 0.0)

                def prep(half, k):
                    b = 2 * half + k
                    if n == 2:
                        dve.wait_ge(s["prep_mm"], b + 1)
                        wait_past(dve, s["prep_hi"], b - 1 + s["block0"])
                        dve.tensor_tensor(fold[k][:], prep_a_ps[k].rearrange("p (c n) -> p c n", c=DC),
                                          bias_col[:, 1, :, None].broadcast_to((P, DC, P)), ALU.add)
                        dve.tensor_tensor(new_h[k][:], prep_b_ps[k][:, 0:D], bias_row[:], ALU.add)\
                           .then_inc(s["prep_fold"], 1)
                        key_src = fold[k][:]
                        value_src = new_h[k][:]
                    else:
                        key_src = prep_a_ps[k].rearrange("p (c n) -> p c n", c=DC)
                        value_src = prep_b_ps[k][:, 0:D]
                    dve.wait_ge(s["prep_hi"], b + 1 + s["block0"])
                    dve.tensor_tensor(keys[:, :, 1, bass.ds(b * P, P)], key_src,
                                      keys[:, :, 0, bass.ds(b * P, P)].bitcast(F32), ALU.subtract)
                    dve.tensor_tensor(values[:, bass.ds(b, 1), 1, :].rearrange("p o d -> p (o d)"), value_src,
                                      values[:, bass.ds(b, 1), 0, :].rearrange("p o d -> p (o d)").bitcast(F32),
                                      ALU.subtract).then_inc(s["prep_lo"], 1)

                blocks(dve, prep)

                def query_fold_part(half, k):
                    b = 2 * half + k
                    dve.wait_ge(s["query_mm"], b + 1)
                    dve.tensor_tensor(fold[k][:], small_ps.rearrange("p (c n) -> p c n", c=DC),
                                      bias_col[:, 0, :, None].broadcast_to((P, DC, P)), ALU.add)\
                       .then_inc(s["query_fold"], 1)

                def query_lo_part(half, k):
                    b = 2 * half + k
                    dve.wait_ge(s["query_hi"], b + 1)
                    if n == 2:
                        dve.scalar_tensor_tensor(out=query_lo[k], in0=fold[k][:], scalar=1.0 / 32,
                                                 in1=query_hi[k].bitcast(F32), op0=ALU.mult,
                                                 op1=ALU.subtract).then_inc(s["query_lo"], 1)
                    else:
                        dve.tensor_tensor(query_lo[k], small_ps.rearrange("p (c n) -> p c n", c=DC),
                                          query_hi[k].bitcast(F32), ALU.subtract).then_inc(s["query_lo"], 1)

                def score_out(half, k, c):
                    b = 2 * half + k
                    j = (NCH * k + c) % 2
                    w = live(c)
                    dve.wait_ge(s["score_mm"], NCH * b + c + 1)
                    wait_past(dve, s["turned"], NCH * (b - 2) + c + 1)
                    top = part[k][:, 0, c:c + 1]
                    if n == 2:
                        dve.wait_ge(s["adj_in"][k], 16 * (half + 1 + s["half0"]))
                        take_wait(k, c)
                        dve.tensor_tensor_reduce(row[k][:, cols(c, w)], score_ps[j][:, 0:w],
                                                 row_in[k][:, cols(c, w)], 2.0, LOW, ALU.add, ALU.max, top)\
                           .then_inc(s["score_out"], 1)
                    else:
                        dve.tensor_scalar(row[k][:, cols(c, w)], score_ps[j][:, 0:w], 1.0, LOW, ALU.mult,
                                          ALU.max, accum_out=top).then_inc(s["score_out"], 1)

                def row_top(half, k):
                    b = 2 * half + k
                    dve.wait_ge(s["score_out"], NCH * (b + 1))
                    link = chained(s["chain"], b)
                    link(dve.tensor_reduce(st(k, 0), part[k][:, 0, :], AX.X, ALU.max))
                    dve.tensor_scalar(st(k, 1), st(k, 0), -1.0, None, ALU.mult).then_inc(s["top"], 1)

                def weigh(half, k, c):
                    b = 2 * half + k
                    w = live(c)
                    if n == 2:
                        return
                    dve.wait_ge(s["exp_done"], NCH * b + c + 1)
                    dve.wait_ge(s["adj_in"][k], 16 * (half + 1 + s["half0"]))
                    dve.tensor_tensor(row[k][:, cols(c, w)], row[k][:, cols(c, w)], row_in[k][:, cols(c, w)],
                                      ALU.mult).then_inc(s["ready"], 1)

                for k in range(2):
                    if n == 2:
                        query_fold_part(0, k)
                    query_lo_part(0, k)
                for c in range(NCH):
                    score_out(0, 0, c)
                row_top(0, 0)
                weigh(0, 0, 0)
                weigh(0, 0, 1)
                lo_part(s, stream(0, 0, 0), 0)

                def epilogue(half, k):
                    b = 2 * half + k
                    link = chained(s["chain2"], {2: 6, 3: 3, 4: 4}[n] * b)
                    link(dve.tensor_reduce(st(k, 17), part[k][:, 1, :], AX.X, ALU.add))
                    link(dve.reciprocal(st(k, 18), st(k, 17)))
                    dve.wait_ge(s["side_done"], b + 1 + s["block0"])
                    dve.wait_ge(s["base_in"][k], 16 * (half + 1 + s["half0"]))
                    if n < 4:
                        wait_stores(s, {2: 3, 3: 2}[n], half, k)
                    else:
                        wait_past(dve, out_stored[k], 16 * half)
                    dve.tensor_tensor(new_x[k][:], sum_ps[k][:, 0:D], side[k][:], ALU.add)\
                       .then_inc(s["sums_read"], 1)
                    dve.wait_ge(s["sums_read"], b + 1 + s["block0"])
                    link(dve.scalar_tensor_tensor(out=new_x[k][:], in0=new_x[k][:], scalar=st(k, 18),
                                                  in1=base[k][:], op0=ALU.mult, op1=ALU.add))
                    if n == 2:
                        variance(link, new_x[k][:], k, s["var"])
                        return
                    leaky = dve.scalar_tensor_tensor(out=new_x[k][:], in0=new_x[k][:], scalar=0.01,
                                                     in1=new_x[k][:], op0=ALU.mult, op1=ALU.max)
                    if n == 3:
                        leaky.then_inc(s["h_done"], 1)
                        return
                    link(leaky)
                    dve.wait_ge(s["extra_in"][k], 16 * (half + 1))
                    dve.tensor_tensor(new_x[k][:], new_x[k][:], side2[k][:], ALU.add).then_inc(s["h_out"], 1)

                def attend(half, k):
                    b = 2 * half + k
                    for c in range(NCH):
                        if not is_last(half, k):
                            for a in SCORES_AT[c]:
                                score_out(*following(half, k), a)
                            if NCH - 1 in SCORES_AT[c]:
                                row_top(*following(half, k))
                        if c + 2 < NCH:
                            weigh(half, k, c + 2)
                        elif not is_last(half, k):
                            weigh(*following(half, k), c + 2 - NCH)
                        if after := chunk_after(half, k, c):
                            lo_part(s, stream(*after), after[2])
                        if not (isinstance(half, int) and b == 0):
                            if c == 1:
                                epilogue(*previous(half, k))
                            if c == 3 and n == 2:
                                epilogue_h(s, *previous(half, k), 6)
                        if c == 5 and not (isinstance(half, int) and half == NB // 2 - 1):
                            if n == 2:
                                query_fold_part(half + 1, k)
                            query_lo_part(half + 1, k)

                blocks(dve, attend)
                epilogue(*end)
                if n == 2:
                    epilogue_h(s, *end, 6)

        @block.gpsimd
        def _(pool):
            pool.wait_ge(consts_set, 2)

            def rstd(arg, done):
                def slot(half, k):
                    pool.wait_ge(arg, 2 * half + k + 1)
                    nc.gpsimd.tensor_tensor(st(k, 13), st(k, 12), minus_half[:, 0:1], ALU.pow).then_inc(done, 1)

                return slot

            s = phases[0]
            for k in range(2):
                of_k = slice(k * NB // 2, (k + 1) * NB // 2)
                pool.wait_ge(s["prep_var"], k + 1)
                nc.gpsimd.tensor_tensor(norm[:, of_k, 3], norm[:, of_k, 2], minus_half[:], ALU.pow)\
                  .then_inc(s["prep_rstd"], 1)

            def mask(half, k):
                b = 2 * half + k
                pool.wait_ge(s["adj_in"][k], 16 * (half + 1 + s["half0"]))
                wait_past(pool, s["turned"], NCH * (b - 1))
                nc.gpsimd.tensor_tensor(spare[k][:, 0:1], minus_half[:, 0:1], minus_half[:, 0:1], ALU.add)
                for c in range(MASKS_POOL):
                    nc.gpsimd.tensor_scalar(row[k][:, cols(c, width(c))], row_in[k][:, cols(c, width(c))], 0.0, None,
                                            ALU.is_gt).then_inc(s["raw_done"], 1)

            def root(half, k):
                pool.wait_ge(s["inverse"], 2 * half + k + 1)
                nc.gpsimd.tensor_tensor(st(k, 15), st(k, 14), plus_half[:], ALU.pow).then_inc(s["root"], 1)

            norm0 = rstd(s["var"], s["rstd"])

            def layer0(half, k):
                if not is_last(half, k):
                    mask(*following(half, k))
                if not (isinstance(half, int) and 2 * half + k == 0):
                    norm0(*previous(half, k))
                if not is_last(half, k):
                    root(*following(half, k))

            pool.wait_ge(s["prep_lo"], NB)
            mask(0, 0)
            root(0, 0)
            blocks(pool, layer0)
            norm0(*end)

            s = phases[1]
            norm1 = rstd(s["var"], s["rstd"])

            def add_right(half, k):
                b = 2 * half + k
                for c in range(NCH):
                    pool.wait_ge(s["raw_done"], NCH * b + c + 1)
                    nc.gpsimd.tensor_tensor(row[k][:, cols(c, width(c))], row[k][:, cols(c, width(c))],
                                            s_right[:, cols(c, width(c))], ALU.add).then_inc(s["arg_done"], 1)

            def layer1(half, k):
                if not is_last(half, k):
                    add_right(*following(half, k))
                if not (isinstance(half, int) and 2 * half + k == 0):
                    norm1(*previous(half, k))

            add_right(0, 0)
            blocks(pool, layer1)
            norm1(*end)

            s = phases[2]
            blocks(pool, rstd(s["var"], s["rstd"]))


def kernel(x, adj, L1_gnn_W_sa, L1_gnn_a_sa, L1_gnn_W_gcnb, L1_gnn_b_gcnb, L1_gnn_Wa, L1_gnn_ba, L1_gnn_Wb,
           L1_gnn_bb, L2_gnn_Wq, L2_gnn_bq, L2_gnn_Wk, L2_gnn_bk, L2_gnn_Wv, L2_gnn_bv, L3_gnn_W_stack):
    import numpy as np
    import concourse.bacc as bacc
    from concourse.bass_utils import run_bass_kernel_spmd

    nc = bacc.Bacc("TRN2", target_bir_lowering=False, num_devices=1)

    def plain(a):
        return np.ascontiguousarray(np.asarray(a))

    x, adj = plain(x), plain(adj)
    x_pad = np.zeros((NP, D), x.dtype)
    x_pad[:N] = x
    x_pad[N:] = x[N - 1:]
    adj_pad = np.zeros((NP, NP), adj.dtype)
    adj_pad[:N, :N] = adj
    adj_pad[N:, :N] = adj[N - 1:]

    def on_all(a):
        return plain(np.tile(plain(a).reshape(1, -1), (P, 1)))

    def by_feature(a):
        return plain(plain(a).reshape(-1, P).T)

    arrays = {
        "in_x": x_pad.reshape(NB, P, D),
        "in_adj": adj_pad,
        "in_eye": np.eye(P, dtype=np.float32),
        "in_w_sa": plain(L1_gnn_W_sa),
        "in_a_sa": on_all(L1_gnn_a_sa),
        "in_w_gcnb": plain(L1_gnn_W_gcnb),
        "in_b_gcnb": on_all(L1_gnn_b_gcnb),
        "in_gate_w": plain(np.stack([by_feature(L1_gnn_Wa), by_feature(L1_gnn_Wb)], axis=1)),
        "in_gate_b": plain(np.concatenate([on_all(L1_gnn_ba), on_all(L1_gnn_bb)], axis=1)),
        "in_w_q": plain(plain(L2_gnn_Wq).T),
        "in_w_k": plain(plain(L2_gnn_Wk).T),
        "in_w_v": plain(plain(L2_gnn_Wv).T),
        "in_b_q": by_feature(L2_gnn_bq),
        "in_b_k": by_feature(L2_gnn_bk),
        "in_b_v": on_all(L2_gnn_bv),
        "in_w_stack": plain(L3_gnn_W_stack),
    }
    args = [nc.dram_tensor(name, a.shape, mybir.dt.from_np(a.dtype), kind="ExternalInput").ap()
            for name, a in arrays.items()]
    out = nc.dram_tensor("out", (NB, P, D), F32, kind="ExternalOutput").ap()
    graph_layers(nc, *args, out)
    result = run_bass_kernel_spmd(nc, [arrays], core_ids=[0])
    return result.results[0]["out"].reshape(NP, D)[:N]
```

```python
from contextlib import ExitStack

import concourse.bass as bass
from concourse import mybir

P = 128
D = 256
DC = D // P
N = 3327
NB = -(-N // P)
NP = NB * P
CW = 512
NCH = -(-NP // CW)
GSTEPS = 2 * NCH
LN_EPS = 1e-5
SIGMOID_FROM = -87.0
LOW = -3.0e38

F32 = mybir.dt.float32
F32R = mybir.dt.float32r
ALU = mybir.AluOpType
ACT = mybir.ActivationFunctionType
AX = mybir.AxisListType

SCORES_AT = [(0, 1), (2, 3), (4,), (5,), (6,), (), ()]
ADJ_FIRST = 4
MASKS_POOL = 4
COUNTS_AT = [(4,), (5, 2), (6, 3), (), (), (), ()]
COUNTS_AT_2 = {5: 0, 6: 1}
assert [c for cs in SCORES_AT for c in cs] == list(range(NCH))


def width(c):
    return min(CW, NP - c * CW)


def live(c):
    return min(CW, N - c * CW)


def cols(c, w):
    return slice(c * CW, c * CW + w)


def wait_past(engine, semaphore, value):
    if isinstance(value, int) and value <= 0:
        return
    engine.wait_ge(semaphore, value)


def blocks(engine, slot):
    pairs = NB // 2
    for k in range(2):
        slot(0, k)
    with engine.Fori(1, pairs - 1) as half:
        for k in range(2):
            slot(half, k)
    for k in range(2):
        slot(pairs - 1, k)


PIECES = [0, 4, 13, 24, 26]
HALF_NB = NB // 2


def prep_blocks(engine, slot, tail=(), arrive=lambda piece: None):
    arrive(0)
    for b in range(4):
        slot(b // 2, b % 2, 0)
        for step in tail[b] if b < len(tail) else ():
            step()
    arrive(1)
    with engine.Fori(2, 6) as half:
        for k in range(2):
            slot(half, k, 0)
    slot(6, 0, 0)
    arrive(2)
    slot(6, 1, 1)
    with engine.Fori(7, 12) as half:
        for k in range(2):
            slot(half, k, 1)
    arrive(3)
    for k in range(2):
        slot(12, k, 1)


def following(half, k):
    return (half, 1) if k == 0 else (half + 1, 0)


def previous(half, k):
    return (half, 0) if k == 1 else (half - 1, 1)


def chunk_after(half, k, c, steps=NCH, by=1):
    if c + by < steps:
        return half, k, c + by
    return None if is_last(half, k) else (*following(half, k), c + by - steps)


def lanes(period, ring, turns_at=()):
    lane = [0, 1]
    for p in range(2, period):
        lane.append(lane[p - 2] if ring == 2 or p in turns_at else 3 - lane[-1] - lane[-2])
    ago = [next(a for a in range(1, period + 1) if lane[(p - a) % period] == lane[p]) for p in range(period)]
    assert min(ago) >= 2
    return lane, ago


AHEAD = 2
TURNS = {(NCH, 2): lanes(2 * NCH, 2), (NCH, 3): lanes(2 * NCH, 3, (5, NCH + 5)),
         (GSTEPS, 3): lanes(2 * GSTEPS, 3, (2 * GSTEPS - 1,))}


def stream(half, k, c, steps=NCH, ring=2):
    lane, ago = TURNS[steps, ring]
    return steps * (2 * half + k) + c, lane[steps * k + c], ago[steps * k + c]


def is_last(half, k):
    return isinstance(half, int) and 2 * half + k == NB - 1


def graph_layers(nc, x, adj, eye, w_sa, a_sa, w_gcnb, b_gcnb, gate_w, gate_b, w_q, w_k, w_v, b_q, b_k,
                 b_v, w_stack, out):
    with ExitStack() as ctx:
        def sb(name, shape, dt=F32):
            return ctx.enter_context(nc.sbuf_tensor(name, shape, dt))

        def sem(name):
            return ctx.enter_context(nc.semaphore(name))

        def sems(name):
            return [sem(f"{name}{k}") for k in range(2)]

        ps = ctx.enter_context(nc.psum_tensor("ps", [P, 8, CW], F32))
        score_ps = [ps[:, k, :] for k in range(2)]
        turn_ps = [ps[:, k, :] for k in (2, 3, 7)]
        sum_ps = [ps[:, 4 + k, :] for k in range(2)]
        small_ps = ps[:, 6, 0:D]
        mix_ps = ps[:, 6, :]

        def turned_h_ps(n):
            return ps[:, 6 if n < 2 else 7, 0:D]

        prep_a_ps = [ps[:, 2, 0:D], ps[:, 0, 0:D]]
        prep_b_ps = [ps[:, 3, :], ps[:, 1, :]]

        values = sb("values", [P, NB, 2, D], F32R)
        keys = sb("keys", [P, DC, 2, NP], F32R)
        values2 = keys[:].rearrange("p a b n -> p (a b n)").rearrange("p (j s d) -> p j s d", s=2, d=D)
        row_in = [sb(f"row_in{k}", [P, NP]) for k in range(2)]
        row = [sb(f"row{k}", [P, NP]) for k in range(2)]
        s_right = sb("s_right", [P, NP])
        s_left = sb("s_left", [P, NB, 2])
        queries = sb("queries", [P, 2, 2, DC, P], F32R)
        query_hi = [queries[:, 0, k] for k in range(2)]
        query_lo = [queries[:, 1, k] for k in range(2)]
        turned_hi = [sb(f"turned_hi{k}", [P, CW], F32R) for k in range(2)]
        turned_lo = [sb(f"turned_lo{k}", [P, CW], F32R) for k in range(2)]
        turned_hi.append(queries[:, 0].rearrange("p k c n -> p (k c n)"))
        turned_lo.append(queries[:, 1].rearrange("p k c n -> p (k c n)"))
        weights = sb("weights", [P, DC, 3 * D])
        ident = sb("ident", [P, P])
        ht_in = [sb(f"ht_in{k}", [P, DC, P]) for k in range(2)]
        base = [sb(f"base{k}", [P, D]) for k in range(2)]
        side = [sb(f"side{k}", [P, D]) for k in range(2)]
        side2 = [sb(f"side2{k}", [P, D]) for k in range(2)]
        new_x = [sb(f"new_x{k}", [P, D]) for k in range(2)]
        new_h = [sb(f"new_h{k}", [P, D]) for k in range(2)]
        new_ht = [sb(f"new_ht{k}", [P, DC, P]) for k in range(2)]
        stat = [sb(f"stat{k}", [P, 40]) for k in range(2)]
        part = [sb(f"part{k}", [P, 2, NCH]) for k in range(2)]
        spare = [sb(f"spare{k}", [P, NCH + 1]) for k in range(2)]
        norm_parts = sb("norm_parts", [P, NB, 6])
        norm = sb("norm", [P, NB, 4])
        minus_half = sb("minus_half", [P, NB // 2])
        plus_half = sb("plus_half", [P, 1])
        bias_row = sb("bias_row", [P, D])
        bias_col = sb("bias_col", [P, 2, DC])
        gate_cols = sb("gate_cols", [P, 2, 4])
        gate_bias = sb("gate_bias", [P, 2])
        fold = [sb(f"fold{k}", [P, DC, P]) for k in range(2)]

        mix_cols = weights[:, :, 0:D]
        sa_cols = weights[:, :, D:2 * D + 1]
        right_cols = weights[:, :, 2 * D + 1:2 * D + 1 + P]
        value_bias = s_right[:, 0:D]
        prep_fold = [(s_right[:, (1 + 2 * k) * D:(2 + 2 * k) * D].rearrange("p (c n) -> p c n", c=DC),
                      s_right[:, (2 + 2 * k) * D:(3 + 2 * k) * D]) for k in range(2)]
        h_0 = [tile[:].rearrange("p (b d) -> p b d", d=D) for tile in (s_right, row[1])]
        a_left, a_right, scratch = side[0][:], side[1][:], new_x[0][:]

        def dram(name, shape):
            return nc.dram_tensor(name, shape, F32, kind="Internal").ap()

        x_mid = [dram(f"x_mid{n}", (NB, P, D)) for n in range(4)]
        h_mid = [dram(f"h_mid{n}", (NB, P, D)) for n in range(3)]
        ht_mid = [dram(f"ht_mid{n}", (NB, P, DC, P)) for n in range(4)]
        adj_rows = adj.rearrange("(b p) n -> b p n", p=P)

        def st(k, a, w=1):
            return stat[k][:, a:a + w]

        consts_in = sem("consts_in")
        consts_set = sem("consts_set")
        out_stored = sems("out_stored")
        shared = {name: sem(name) for name in (
            "prep_hi", "prep_lo",
            "side_done", "sums_read")}
        shared["stage_set"] = sem("stage_set")
        shared.update({name: sems(name) for name in ("adj_in", "adj_rest", "base_in", "ht_in")})
        shared["ht_piece"] = [sem(f"ht_piece{i}") for i in range(4)]
        frame = ["ready", "turned", "hi_done", "lo_done", "multiplied",
                 "chain2"]
        normed = ["var", "rstd"]
        features = ["h_done", "h_turned", "h_out"]
        attention = ["wts_in", "prep_mm", "query_mm", "query_hi", "query_lo",
                     "score_mm", "score_out", "top", "exp_done", "chain"]
        own_pairs = [["stored"], ["stored"], ["stored"], ["stored"], ["extra_in"]]
        own = [
            normed + features + ["prep_var", "prep_rstd", "prep_h", "prep_chain", "raw_done", "relu_done", "count_done",
                                 "inverse", "root", "chain"],
            normed + features + ["wts_in", "wts_set", "prep_mm", "prep_chain", "raw_done", "arg_done",
                                 "exp_done", "left_here", "ts_done", "ts_turned", "ts_out", "mix_mm", "gate_arg",
                                 "gate_exp", "sig_arg", "sig_tanh"],
            normed + features + attention + ["prep_fold", "query_fold", "wq_in"],
            features + attention,
            ["h_out"] + attention,
        ]
        phases = []
        for n in range(5):
            named = {name: sem(f"{name}_{n}") for name in frame + own[n]}
            named.update({name: sems(f"{name}_{n}_") for name in own_pairs[n]})
            phases.append({**shared, **named, "layer": n, "block0": NB * n, "half0": NB // 2 * n,
                           "half1": NB // 2 * (n - 1),
                           "block1": NB * (n - 1)})
        phases[0]["x_in"] = [sem(f"x_in{i}") for i in range(2)]
        phases[1]["h_piece"] = [sem(f"h_piece{i}") for i in range(4)]

        block = ctx.enter_context(nc.Block())

        end = (NB // 2 - 1, 1)

        def alone(engine):
            engine.wait_ge(consts_in, 16)

        def wait_adj(engine, s, half, k, c):
            part_in = s["adj_in"] if c < ADJ_FIRST else s["adj_rest"]
            engine.wait_ge(part_in[k], 16 * (half + 1 + s["half0"]))

        @block.sync
        def _(sp):
            sp.dma_start(ident[:], eye).then_inc(consts_in, 16)

            def at(array, b):
                if isinstance(b, int):
                    return array[b]
                view = array[bass.ds(b, 1)]
                names = " ".join("cde"[:len(array.shape) - 2])
                return view.rearrange(f"o p {names} -> (o p) {names}")

            def load_adj(s, half, k, before=lambda part: None):
                b = 2 * half + k
                for part_of, (lo, hi) in enumerate(((0, ADJ_FIRST * CW), (ADJ_FIRST * CW, NP))):
                    before(part_of)
                    part_in = (s["adj_in"], s["adj_rest"])[part_of]
                    sp.dma_start(row_in[k][:, lo:hi], at(adj_rows, b)[:, lo:hi]).then_inc(part_in[k], 16)

            def load_piece(tiles, array, i, semaphore):
                sp.dma_start(tiles, array[PIECES[i]:PIECES[i + 1]].rearrange("b p c n -> p b c n"))\
                  .then_inc(semaphore[i], 16)

            def load_ht_piece(n, i):
                tile = i // 2
                lo, hi = (D * (PIECES[i + e] - tile * HALF_NB) for e in range(2))
                load_piece(row[tile][:, lo:hi].rearrange("p (b c n) -> p b c n", c=DC, n=P), ht_mid[n - 1], i,
                           phases[n]["ht_piece"])

            def load_h_piece(i):
                b0, b1 = PIECES[i], PIECES[i + 1]
                sp.dma_start(values[:, b0:b1, 1, :].bitcast(F32), h_mid[0][b0:b1].rearrange("b p d -> p b d"))\
                  .then_inc(phases[1]["h_piece"][i], 16)

            def layer_loads(n, base_from, ht_from, stores, freed_by, per, freed_after, extra_from=None,
                            next_weights=lambda: None):
                s = phases[n]
                steps = GSTEPS if n == 1 else NCH

                def load_adj_2(half, k):
                    b = 2 * half + k

                    def before(part_of):
                        sp.wait_ge(s[freed_by], per * (b - 2) + freed_after[part_of])

                    if isinstance(half, int) and b >= NB:
                        load_adj(s, half - NB // 2, k, before)
                    else:
                        load_adj(s, half, k, before)

                def load_ht(half, k):
                    if n >= 2:
                        wait_past(sp, s["query_mm"], 2 * half + k - 1)
                    else:
                        wait_past(sp, s["mix_mm"], 2 * half + k - 1)
                    sp.dma_start(ht_in[k][:], at(ht_from, 2 * half + k)).then_inc(s["ht_in"][k], 16)

                def store(half, k):
                    b = 2 * half + k
                    sp.wait_ge(s["h_out"], b + 1)
                    if n == 4:
                        sp.dma_start(at(out, b), new_x[k][:]).then_inc(out_stored[k], 16)
                        return
                    for tile, array in stores:
                        sp.dma_start(at(array, b), tile[k][:]).then_inc(s["stored"][k], 16)

                def stored_until(b):
                    for k in range(2):
                        sp.wait_ge(s["stored"][k], 16 * len(stores) * ((b + 1 - k) // 2))

                if ht_from is not None:
                    sp.wait_ge(s["prep_mm"], NB)
                    for k in range(2):
                        load_ht(0, k)

                def slot(half, k):
                    b = 2 * half + k
                    final = isinstance(half, int) and half == NB // 2 - 1
                    wait_past(sp, s["h_out"], b - 1)
                    sp.dma_start(base[k][:], at(base_from, b)).then_inc(s["base_in"][k], 16)
                    if extra_from is not None:
                        sp.dma_start(side2[k][:], at(extra_from, b)).then_inc(s["extra_in"][k], 16)
                    if final and k == 1 and n < 4:
                        next_weights()
                        sp.wait_ge(s["turned"], steps * (NB - 1))
                        stored_until(PIECES[2])
                        load_ht_piece(n + 1, 0)
                        load_ht_piece(n + 1, 1)
                    if not final:
                        if ht_from is not None:
                            load_ht(half + 1, k)
                    if not (final and n == 4):
                        load_adj_2(half + 1, k)
                    if isinstance(half, int) and b == 0:
                        return
                    store(*previous(half, k))

                blocks(sp, slot)
                if n == 0:
                    sp.wait_ge(s["multiplied"], steps * NB)
                    load_h_piece(0)
                    load_h_piece(1)
                if n < 4:
                    sp.wait_ge(s["turned"], steps * NB)
                    stored_until(PIECES[3])
                    load_ht_piece(n + 1, 2)
                if n == 0:
                    load_h_piece(2)
                store(NB // 2 - 1, 1)
                if n < 4:
                    stored_until(NB)
                    load_ht_piece(n + 1, 3)
                if n == 0:
                    load_h_piece(3)

            for i in range(2):
                of_i = slice(i * HALF_NB, (i + 1) * HALF_NB)
                sp.dma_start(h_0[i], x[of_i].rearrange("b p d -> p b d")).then_inc(phases[0]["x_in"][i], 16)
            for i in range(2):
                load_adj(phases[0], 0, i)

            s = phases[1]
            rows_of = "(c p) n -> p c n"
            sp.dma_start(mix_cols, w_gcnb.rearrange(rows_of, p=P)).then_inc(s["wts_in"], 16)
            sp.dma_start(sa_cols[:, :, 0:D], w_sa.rearrange(rows_of, p=P)).then_inc(s["wts_in"], 16)
            sp.dma_start(a_left, a_sa[:, 0:D]).then_inc(s["wts_in"], 16)
            sp.dma_start(a_right, a_sa[:, D:2 * D]).then_inc(s["wts_in"], 16)
            sp.dma_start(bias_row[:], b_gcnb).then_inc(s["wts_in"], 16)
            sp.dma_start(gate_cols[:], gate_w).then_inc(s["wts_in"], 16)
            sp.dma_start(gate_bias[:], gate_b).then_inc(s["wts_in"], 16)
            sp.dma_start(bias_col[:, 0, :], b_q).then_inc(s["wts_in"], 16)
            sp.dma_start(bias_col[:, 1, :], b_k).then_inc(s["wts_in"], 16)

            by_chunk = (ADJ_FIRST, NCH)
            layer_loads(0, x, None, [(new_x, x_mid[0]), (new_h, h_mid[0]), (new_ht, ht_mid[0])],
                        "ready", NCH, by_chunk)

            def weights_2():
                sp.wait_ge(phases[1]["arg_done"], NCH * NB)
                s = phases[2]
                for i, w in ((1, w_k), (2, w_v)):
                    sp.dma_start(weights[:, :, i * D:(i + 1) * D], w.rearrange(rows_of, p=P)).then_inc(s["wts_in"], 16)
                sp.dma_start(value_bias, b_v).then_inc(s["wts_in"], 16)

            layer_loads(1, x_mid[0], ht_mid[0], [(new_x, x_mid[1]), (new_ht, ht_mid[1])],
                        "turned", GSTEPS, by_chunk, next_weights=weights_2)

            sp.wait_ge(phases[1]["mix_mm"], NB)
            sp.dma_start(weights[:, :, 0:D], w_q.rearrange(rows_of, p=P)).then_inc(phases[2]["wq_in"], 16)

            def weights_3(n):
                def load():
                    sp.wait_ge(phases[n - 1]["query_mm"], NB)
                    sp.dma_start(weights[:, :, 0:2 * D], w_stack[n - 3].rearrange(rows_of, p=P))\
                      .then_inc(phases[n]["wts_in"], 16)

                return load

            layer_loads(2, x_mid[1], ht_mid[1], [(new_x, x_mid[2]), (new_h, h_mid[1]), (new_ht, ht_mid[2])],
                        "score_out", NCH, by_chunk, next_weights=weights_3(3))
            layer_loads(3, h_mid[1], ht_mid[2], [(new_x, h_mid[2]), (new_ht, ht_mid[3])],
                        "ready", NCH, by_chunk, next_weights=weights_3(4))
            layer_loads(4, h_mid[2], ht_mid[3], [], "ready", NCH, by_chunk, extra_from=x_mid[2])
            for k in range(2):
                sp.wait_ge(out_stored[k], 16 * (NB // 2))

        @block.tensor
        def _(pe):
            pe.wait_ge(consts_in, 16)

            def turn(s, src, g, c, source_ready):
                value, j, ago = g
                wait_past(pe, s["lo_done"], value - ago + 1)
                source_ready()
                for i in range(width(c) // P):
                    mm = pe.transpose(turn_ps[j][:, i * P:(i + 1) * P], src[:, c * CW + i * P:c * CW + (i + 1) * P],
                                      ident[:])
                mm.then_inc(s["turned"], 1)

            def multiply(s, bank, vals, g, c):
                value, j, _ = g
                pe.wait_ge(s["lo_done"], value + 1)
                for i in range(width(c) // P):
                    jb = c * (CW // P) + i
                    pe.matmul(bank, turned_hi[j][:, i * P:(i + 1) * P],
                              vals[:, jb, :, :].rearrange("p s d -> p (s d)"),
                              start=(jb == 0), stop=False, skip_group_check=True)
                    mm = pe.matmul(bank[:, 0:D], turned_lo[j][:, i * P:(i + 1) * P], vals[:, jb, 0, :],
                                   start=False, stop=(jb == NB - 1), skip_group_check=True)
                mm.then_inc(s["multiplied"], 1)

            def turn_h(s, half, k):
                pe.wait_ge(s["h_done"], 2 * half + k + 1)
                src = new_x[k] if s["layer"] == 3 else new_h[k]
                for i in range(DC):
                    mm = pe.transpose(turned_h_ps(s["layer"])[:, i * P:(i + 1) * P], src[:, i * P:(i + 1) * P], ident[:])
                mm.then_inc(s["h_turned"], 1)

            s = phases[0]
            pe.wait_ge(s["prep_lo"], NB + s["block0"])

            def turn_row(s, half, k, c, ring=2):
                turn(s, row[k], stream(half, k, c, ring=ring), c,
                     lambda: pe.wait_ge(s["ready"], NCH * (2 * half + k) + c + 1))

            def layer0(half, k):
                b = 2 * half + k
                wait_past(pe, s["sums_read"], b - 1 + s["block0"])
                for c in range(NCH):
                    if after := chunk_after(half, k, c, by=AHEAD):
                        turn_row(s, *after, ring=3)
                    multiply(s, sum_ps[k], values, stream(half, k, c, ring=3), c)
                    if c == 5 and not (isinstance(half, int) and b == 0):
                        turn_h(s, *previous(half, k))

            for c in range(AHEAD):
                turn_row(s, 0, 0, c, ring=3)
            blocks(pe, layer0)

            s = phases[1]
            pe.wait_ge(s["wts_set"], 1)

            def stage_wait(s, half, k):
                b = 2 * half + k
                pe.wait_ge(s["stage_set"], b + 1 + s["block1"])
                if isinstance(half, int) and b < 2:
                    if b == 1:
                        pe.wait_ge(s["sums_read"], s["block0"])
                    return
                if s["layer"] == 2:
                    pe.wait_ge(s["prep_fold"], b - 1)
                else:
                    pe.wait_ge(s["prep_lo"], b - 1 + s["block0"])

            def prep1(half, k, tile):
                stage_wait(s, half, k)
                for i in range(DC):
                    pe.matmul(prep_b_ps[k][:, 0:D + 1], ht_in[k][:, i, :], sa_cols[:, i, :], start=(i == 0),
                              stop=(i == DC - 1))
                for i in range(DC):
                    mm = pe.matmul(prep_a_ps[k][:, 0:P], right_cols[:, i, :], ht_in[k][:, i, :],
                                   start=(i == 0), stop=(i == DC - 1))
                mm.then_inc(s["prep_mm"], 1)

            prep_blocks(pe, prep1, [[], [], [lambda: turn_h(phases[0], *end)]])
            pe.wait_ge(s["prep_lo"], NB + s["block0"])

            def turn_step(half, k, g):
                if g < NCH:
                    turn(s, row_in[k], stream(half, k, g, GSTEPS, 3), g,
                         lambda: wait_adj(pe, s, half, k, g))
                else:
                    turn(s, row[k], stream(half, k, g, GSTEPS, 3), g - NCH,
                         lambda: pe.wait_ge(s["ready"], NCH * (2 * half + k) + g - NCH + 1))

            def layer1(half, k):
                b = 2 * half + k
                wait_past(pe, s["sums_read"], b - 1 + s["block0"])
                for g in range(GSTEPS):
                    if after := chunk_after(half, k, g, GSTEPS, AHEAD):
                        turn_step(*after)
                    if g < NCH:
                        multiply(s, sum_ps[k], values, stream(half, k, g, GSTEPS, 3), g)
                    else:
                        multiply(s, score_ps[k], values2, stream(half, k, g, GSTEPS, 3), g - NCH)
                    if not (isinstance(half, int) and b == 0):
                        if g == 3:
                            turn_ts(*previous(half, k))
                        if g == 4:
                            mix(*previous(half, k))
                        if g == 12:
                            turn_h(s, *previous(half, k))

            def turn_ts(half, k):
                s = phases[1]
                wait_past(pe, s["h_out"], 2 * half + k)
                pe.wait_ge(s["ts_done"], 2 * half + k + 1)
                for i in range(DC):
                    mm = pe.transpose(small_ps[:, i * P:(i + 1) * P], side2[k][:, i * P:(i + 1) * P], ident[:])
                mm.then_inc(s["ts_turned"], 1)

            def mix(half, k):
                s = phases[1]
                pe.wait_ge(s["ts_out"], 2 * half + k + 1)
                pe.wait_ge(s["ht_in"][k], 16 * (half + 1 + s["half1"]))
                for i in range(DC):
                    pe.matmul(mix_ps[:, 0:D], fold[k][:, i, :], mix_cols[:, i, :], start=(i == 0), stop=False,
                              skip_group_check=True)
                for i in range(DC):
                    pe.matmul(mix_ps[:, D:D + 2], fold[k][:, i, :], gate_cols[:, :, i], start=False, stop=False,
                              skip_group_check=True)
                for i in range(DC):
                    mm = pe.matmul(mix_ps[:, D:D + 2], ht_in[k][:, i, :], gate_cols[:, :, 2 + i], start=False,
                                   stop=(i == DC - 1), skip_group_check=True)
                mm.then_inc(s["mix_mm"], 1)

            for g in range(AHEAD):
                turn_step(0, 0, g)
            blocks(pe, layer1)

            for n in (2, 3, 4):
                s = phases[n]
                key_at = D
                value_at = 2 * D if n == 2 else 0
                pe.wait_ge(s["wts_in"], 16 * (3 if n == 2 else 1))

                def prep(half, k, tile):
                    stage_wait(s, half, k)
                    for o in range(DC):
                        for i in range(DC):
                            pe.matmul(prep_a_ps[k][:, o * P:(o + 1) * P],
                                      weights[:, i, key_at + o * P:key_at + (o + 1) * P], ht_in[k][:, i, :],
                                      start=(i == 0), stop=(i == DC - 1))
                    for i in range(DC):
                        mm = pe.matmul(prep_b_ps[k][:, 0:D], ht_in[k][:, i, :],
                                       weights[:, i, value_at:value_at + D], start=(i == 0), stop=(i == DC - 1))
                    mm.then_inc(s["prep_mm"], 1)

                last_turn = lambda: turn_h(phases[n - 1], *end)
                if n == 2:
                    tail = [[lambda: turn_ts(*end), lambda: mix(*end)], [], [], [last_turn]]
                else:
                    tail = [[], [], [last_turn]]
                prep_blocks(pe, prep, tail)
                pe.wait_ge(s["prep_lo"], NB + s["block0"])
                if n == 2:
                    pe.wait_ge(s["wq_in"], 16)

                def query(half, k):
                    b = 2 * half + k
                    pe.wait_ge(s["ht_in"][k], 16 * (half + 1 + s["half1"]))
                    wait_past(pe, s["query_lo"], b)
                    for o in range(DC):
                        for i in range(DC):
                            mm = pe.matmul(small_ps[:, o * P:(o + 1) * P], weights[:, i, o * P:(o + 1) * P],
                                           ht_in[k][:, i, :], start=(i == 0), stop=(i == DC - 1))
                    mm.then_inc(s["query_mm"], 1)

                def scores(half, k, c):
                    b = 2 * half + k
                    j = (NCH * k + c) % 2
                    pe.wait_ge(s["query_lo"], b + 1)
                    wait_past(pe, s["score_out"], NCH * b + c - 1)
                    w = width(c)
                    for i in range(DC):
                        for q, side_of_key in ((query_hi, 0), (query_hi, 1), (query_lo, 0)):
                            mm = pe.matmul(score_ps[j][:, 0:w], q[k][:, i, :], keys[:, i, side_of_key, cols(c, w)],
                                           start=(i == 0 and q is query_hi and side_of_key == 0),
                                           stop=(i == DC - 1 and q is query_lo))
                    mm.then_inc(s["score_mm"], 1)

                query(0, 0)
                query(0, 1)
                for c in range(NCH):
                    scores(0, 0, c)

                turn_row(s, 0, 0, 0)

                def attend(half, k):
                    b = 2 * half + k
                    wait_past(pe, s["sums_read"], b - 1 + s["block0"])
                    for c in range(NCH):
                        if not is_last(half, k):
                            for a in SCORES_AT[c]:
                                scores(*following(half, k), a)
                        if after := chunk_after(half, k, c):
                            turn_row(s, *after)
                        multiply(s, sum_ps[k], values, stream(half, k, c), c)
                        if c == 4 and not (isinstance(half, int) and b == 0) and n < 4:
                            turn_h(s, *previous(half, k))
                        if c == 5 and not (isinstance(half, int) and half == NB // 2 - 1):
                            query(half + 1, k)

                blocks(pe, attend)

        @block.scalar
        def _(act):
            def hi_part(s, g, c):
                value, j, ago = g
                act.wait_ge(s["turned"], value + 1)
                wait_past(act, s["multiplied"], value - ago + 1)
                act.activation(turned_hi[j][:, 0:width(c)], turn_ps[j][:, 0:width(c)], ACT.Copy)\
                   .then_inc(s["hi_done"], 1)

            def side_copy(s, half, k):
                b = 2 * half + k
                steps = GSTEPS if s["layer"] == 1 else NCH
                act.wait_ge(s["multiplied"], steps * (b + 1))
                wait_past(act, s["sums_read"], b - 1 + s["block0"])
                if s["layer"] == 1:
                    act.activation(new_h[k][:], score_ps[k][:, D:2 * D], ACT.Copy)
                act.activation(side[k][:], sum_ps[k][:, D:2 * D], ACT.Copy).then_inc(s["side_done"], 1)

            def ht_copy(s, half, k):
                b = 2 * half + k
                act.wait_ge(s["h_turned"], b + 1)
                stores = {0: 3, 1: 2, 2: 3, 3: 2}[s["layer"]]
                wait_past(act, s["stored"][k], 16 * stores * half)
                act.activation(new_ht[k][:].rearrange("p c n -> p (c n)"), turned_h_ps(s["layer"]), ACT.Copy)\
                   .then_inc(s["h_out"], 1)

            s = phases[0]

            for i in range(2):
                of_i = slice(i * HALF_NB, (i + 1) * HALF_NB)
                act.wait_ge(s["prep_h"], i + 1)
                act.activation(values[:, of_i, 0, :], h_0[i], ACT.Relu).then_inc(s["prep_hi"], HALF_NB)

            def count(half, k, c):
                b = 2 * half + k
                tile = row[k][:, cols(c, width(c))]
                if c < MASKS_POOL:
                    act.wait_ge(s["raw_done"], MASKS_POOL * b + c + 1)
                    act.activation(tile, tile, ACT.Copy, accum_out=part[k][:, 0, c:c + 1])\
                       .then_inc(s["count_done"], 1)
                    return
                wait_adj(act, s, half, k, c)
                wait_past(act, s["turned"], NCH * (b - 2) + c + 1)
                act.activation(tile, row_in[k][:, cols(c, width(c))], ACT.Relu).then_inc(s["relu_done"], 1)
                act.wait_ge(s["relu_done"], (NCH - MASKS_POOL) * b + c - MASKS_POOL + 1)
                act.activation(tile, tile, ACT.Sign, accum_out=part[k][:, 0, c:c + 1])\
                   .then_inc(s["count_done"], 1)

            for a in range(NCH):
                count(0, 0, a)
            act.wait_ge(s["prep_lo"], NB)

            def layer0(half, k):
                b = 2 * half + k
                for c in range(NCH):
                    if after := chunk_after(half, k, c, by=AHEAD):
                        hi_part(s, stream(*after, ring=3), after[2])
                    if not is_last(half, k):
                        if isinstance(half, int) and b == 0 and c == 0:
                            for a in COUNTS_AT_2.values():
                                count(*following(half, k), a)
                        for a in COUNTS_AT[c]:
                            count(*following(half, k), a)
                    if c in COUNTS_AT_2 and not (isinstance(half, int) and half == NB // 2 - 1):
                        count(half + 1, k, COUNTS_AT_2[c])
                    if not (isinstance(half, int) and b == 0):
                        if c == 0:
                            side_copy(s, *previous(half, k))
                        if c == 6:
                            ht_copy(s, *previous(half, k))

            for c in range(AHEAD):
                hi_part(s, stream(0, 0, c, ring=3), c)
            blocks(act, layer0)
            side_copy(s, *end)

            s = phases[1]

            def prep1(half, k, tile):
                b = 2 * half + k
                act.activation(values[:, bass.ds(b, 1), 0, :].rearrange("p o d -> p (o d)"),
                               values[:, bass.ds(b, 1), 1, :].rearrange("p o d -> p (o d)").bitcast(F32), ACT.Copy)
                act.wait_ge(s["prep_mm"], b + 1)
                alone(act)
                act.activation(s_right[:, bass.ds(b * P, P)], prep_a_ps[k][:, 0:P], ACT.Copy)
                act.activation(values2[:, bass.ds(b, 1), 0, :].rearrange("p o d -> p (o d)"),
                               prep_b_ps[k][:, 0:D], ACT.Copy).then_inc(s["prep_hi"], 1)

            prep_blocks(act, prep1, [[], [], [lambda: ht_copy(phases[0], *end)]],
                        lambda i: act.wait_ge(s["h_piece"][i], 16))
            act.wait_ge(s["prep_lo"], NB + s["block0"])

            def positive_part(half, k, c):
                b = 2 * half + k
                if c == 0:
                    act.wait_ge(s["left_here"], b + 1)
                wait_past(act, s["turned"], GSTEPS * (b - 2) + NCH + c + 1)
                act.activation(row[k][:, cols(c, width(c))], s_right[:, cols(c, width(c))], ACT.Relu,
                               bias=st(k, 26), scale=99.0).then_inc(s["raw_done"], 1)

            def exponential(half, k, c):
                b = 2 * half + k
                act.wait_ge(s["arg_done"], NCH * b + c + 1)
                act.activation(row[k][:, cols(c, width(c))], row[k][:, cols(c, width(c))], ACT.Exp,
                               bias=st(k, 27), scale=-0.01).then_inc(s["exp_done"], 1)

            def ts_copy(half, k):
                s = phases[1]
                act.wait_ge(s["ts_turned"], 2 * half + k + 1)
                act.activation(fold[k][:].rearrange("p c n -> p (c n)"), small_ps, ACT.Copy).then_inc(s["ts_out"], 1)

            def gate_exp(half, k):
                s = phases[1]
                act.wait_ge(s["gate_arg"], 2 * half + k + 1)
                act.activation(st(k, 2, 2), st(k, 0, 2), ACT.Exp, scale=-1.0).then_inc(s["gate_exp"], 1)

            def sig_tanh(half, k):
                s = phases[1]
                act.wait_ge(s["sig_arg"], 2 * half + k + 1)
                act.activation(side[k][:], side2[k][:], ACT.Tanh, scale=0.5).then_inc(s["sig_tanh"], 1)

            def layer1(half, k):
                b = 2 * half + k
                for g in range(GSTEPS):
                    if after := chunk_after(half, k, g, GSTEPS, AHEAD):
                        hi_part(s, stream(*after, GSTEPS, 3), after[2] % NCH)
                    if isinstance(half, int) and b == 0:
                        for c in (2 * g, 2 * g + 1):
                            if c < NCH:
                                exponential(0, 0, c)
                    if not is_last(half, k):
                        if g < NCH:
                            positive_part(*following(half, k), g)
                        else:
                            exponential(*following(half, k), g - NCH)
                    if not (isinstance(half, int) and b == 0):
                        prev = previous(half, k)
                        if g == 0:
                            side_copy(s, *prev)
                        if g == 3:
                            ts_copy(*prev)
                        if g == 5:
                            gate_exp(*prev)
                        if g == 7:
                            sig_tanh(*prev)
                        if g == 13:
                            ht_copy(s, *prev)

            for g in range(AHEAD):
                hi_part(s, stream(0, 0, g, GSTEPS, 3), g)
            for c in range(NCH):
                positive_part(0, 0, c)
            blocks(act, layer1)
            side_copy(s, *end)

            for n in (2, 3, 4):
                s = phases[n]

                def prep(half, k, tile):
                    b = 2 * half + k
                    if n == 2:
                        act.wait_ge(s["prep_fold"], b + 1)
                        key_src, value_src = prep_fold[k]
                    else:
                        act.wait_ge(s["prep_mm"], b + 1)
                        key_src = prep_a_ps[k].rearrange("p (c n) -> p c n", c=DC)
                        value_src = prep_b_ps[k][:, 0:D]
                    alone(act)
                    act.activation(keys[:, :, 0, bass.ds(b * P, P)], key_src, ACT.Copy)
                    act.activation(values[:, bass.ds(b, 1), 0, :].rearrange("p o d -> p (o d)"), value_src,
                                   ACT.Copy).then_inc(s["prep_hi"], 1)

                last_copy = lambda: ht_copy(phases[n - 1], *end)
                if n == 2:
                    tail = [[lambda: ts_copy(*end)], [lambda: gate_exp(*end)], [lambda: sig_tanh(*end)], [last_copy]]
                else:
                    tail = [[], [], [last_copy]]
                prep_blocks(act, prep, tail)

                def query_hi_part(half, k):
                    b = 2 * half + k
                    wait_past(act, s["score_mm"], NCH * (b - 1))
                    if n == 2:
                        act.wait_ge(s["query_fold"], b + 1)
                        act.activation(query_hi[k], fold[k][:], ACT.Copy, scale=1.0 / 32)\
                           .then_inc(s["query_hi"], 1)
                    else:
                        act.wait_ge(s["query_mm"], b + 1)
                        act.activation(query_hi[k], small_ps.rearrange("p (c n) -> p c n", c=DC), ACT.Copy)\
                           .then_inc(s["query_hi"], 1)

                query_hi_part(0, 0)
                query_hi_part(0, 1)

                def exponential(half, k, c):
                    b = 2 * half + k
                    if c == 0:
                        act.wait_ge(s["top"], b + 1)
                    act.activation(row[k][:, cols(c, live(c))], row[k][:, cols(c, live(c))], ACT.Exp,
                                   bias=st(k, 1), accum_out=part[k][:, 1, c:c + 1])\
                       .then_inc(s["ready"] if n == 2 else s["exp_done"], 1)

                def attend(half, k):
                    b = 2 * half + k
                    for c in range(NCH):
                        if c + 2 < NCH:
                            exponential(half, k, c + 2)
                        elif not is_last(half, k):
                            exponential(*following(half, k), c + 2 - NCH)
                        if after := chunk_after(half, k, c):
                            hi_part(s, stream(*after), after[2])
                        if not (isinstance(half, int) and b == 0):
                            if c == 0:
                                side_copy(s, *previous(half, k))
                            if c == 4 and n < 4:
                                ht_copy(s, *previous(half, k))
                        if c == 5 and not (isinstance(half, int) and half == NB // 2 - 1):
                            query_hi_part(half + 1, k)

                exponential(0, 0, 0)
                exponential(0, 0, 1)
                hi_part(s, stream(0, 0, 0), 0)
                blocks(act, attend)
                side_copy(s, *end)

        @block.vector
        def _(dve):
            nc.vector.memset(minus_half[:], -0.5).then_inc(consts_set, 1)
            nc.vector.memset(plus_half[:], 0.5).then_inc(consts_set, 1)

            def chained(semaphore, before):
                done = [0]

                def link(instruction):
                    done[0] += 1
                    instruction.then_inc(semaphore, 1)
                    dve.wait_ge(semaphore, before + done[0])

                return link

            def lo_part(s, g, c):
                value, j, ago = g
                dve.wait_ge(s["hi_done"], value + 1)
                wait_past(dve, s["multiplied"], value - ago + 1)
                dve.tensor_tensor(turned_lo[j][:, 0:width(c)], turn_ps[j][:, 0:width(c)],
                                  turned_hi[j][:, 0:width(c)].bitcast(F32), ALU.subtract).then_inc(s["lo_done"], 1)

            def take_wait(k, column):
                dve.memset(spare[k][:, column:column + 1], 0.0)

            def variance(link, src, k, semaphore):
                link(dve.bn_stats(st(k, 4, 6), src))
                take_wait(k, NCH)
                link(dve.bn_aggr(st(k, 10, 2), st(k, 4, 6)))
                dve.tensor_scalar(st(k, 12), st(k, 11), LN_EPS, None, ALU.add).then_inc(semaphore, 1)

            def relu_norm(link, src, k, rstd_ready, semaphore):
                rstd_ready()
                link(dve.tensor_scalar(new_h[k][:], src, st(k, 10), st(k, 13), ALU.subtract, ALU.mult))
                dve.tensor_scalar(new_h[k][:], new_h[k][:], 0.0, None, ALU.max).then_inc(semaphore, 1)

            s = phases[0]

            link = chained(s["prep_chain"], 0)
            for i in range(2):
                dve.wait_ge(s["x_in"][i], 16)
                for j in range(HALF_NB):
                    b = i * HALF_NB + j
                    last = dve.bn_stats(norm_parts[:, b, :], h_0[i][:, j, :])
                link(last)
                for j in range(HALF_NB):
                    b = i * HALF_NB + j
                    last = dve.bn_aggr(norm[:, b, 0:2], norm_parts[:, b, :])
                link(last)
                of_i = slice(i * HALF_NB, (i + 1) * HALF_NB)
                dve.tensor_scalar(norm[:, of_i, 2], norm[:, of_i, 1], LN_EPS, None, ALU.add).then_inc(s["prep_var"], 1)
            for i in range(2):
                dve.wait_ge(s["prep_rstd"], i + 1)
                for j in range(HALF_NB):
                    b = i * HALF_NB + j
                    last = dve.tensor_scalar(h_0[i][:, j, :], h_0[i][:, j, :], norm[:, b, 0:1], norm[:, b, 3:4],
                                             ALU.subtract, ALU.mult)
                last.then_inc(s["prep_h"], 1)
            for i in range(2):
                dve.wait_ge(s["prep_hi"], (i + 1) * HALF_NB)
                of_i = slice(i * HALF_NB, (i + 1) * HALF_NB)
                dve.scalar_tensor_tensor(out=values[:, of_i, 1, :], in0=h_0[i], scalar=0.0,
                                         in1=values[:, of_i, 0, :].bitcast(F32), op0=ALU.max, op1=ALU.subtract)\
                   .then_inc(s["prep_lo"], HALF_NB)

            dve.wait_ge(phases[1]["wts_in"], 9 * 16)
            link = chained(phases[1]["prep_chain"], 0)
            for i in range(DC):
                link(dve.tensor_tensor_reduce(scratch, sa_cols[:, i, 0:D], a_left, 1.0, 0.0, ALU.mult,
                                              ALU.add, sa_cols[:, i, D:D + 1]))
                link(dve.tensor_tensor_reduce(scratch, sa_cols[:, i, 0:D], a_right, 1.0, 0.0, ALU.mult,
                                              ALU.add, st(0, 20 + i)))
            link(dve.memset(scratch[:, 0:P], 1.0))
            for i in range(DC):
                last = dve.tensor_scalar(right_cols[:, i, :], scratch[:, 0:P], st(0, 20 + i), None, ALU.mult)
            last.then_inc(phases[1]["wts_set"], 1)

            def degree_count(half, k):
                b = 2 * half + k
                dve.wait_ge(s["count_done"], NCH * (b + 1))
                dve.tensor_reduce(st(k, 14), part[k][:, 0, :], AX.X, ALU.add).then_inc(s["inverse"], 1)

            def inverse_norm(half, k):
                b = 2 * half + k
                link = chained(s["chain"], 2 * b)
                dve.wait_ge(s["root"], b + 1)
                link(dve.tensor_scalar(st(k, 16), st(k, 15), 1e-12, None, ALU.max))
                link(dve.reciprocal(st(k, 16), st(k, 16)))

            def incidence(half, k, c):
                w = width(c)
                dve.scalar_tensor_tensor(out=row[k][:, cols(c, w)], in0=row[k][:, cols(c, w)], scalar=st(k, 16),
                                         in1=row_in[k][:, cols(c, w)], op0=ALU.mult, op1=ALU.add,
                                         accum_out=part[k][:, 1, c:c + 1]).then_inc(s["ready"], 1)

            def epilogue0_sums(half, k):
                b = 2 * half + k
                link = chained(s["chain2"], 6 * b)
                link(dve.tensor_reduce(st(k, 17), part[k][:, 1, :], AX.X, ALU.add))
                link(dve.reciprocal(st(k, 18), st(k, 17)))
                dve.wait_ge(s["side_done"], b + 1 + s["block0"])
                wait_stores(s, 3, half, k)
                dve.tensor_tensor(new_x[k][:], sum_ps[k][:, 0:D], side[k][:], ALU.add).then_inc(s["sums_read"], 1)

            def epilogue0(half, k):
                b = 2 * half + k
                link = chained(s["chain2"], 6 * b + 2)
                dve.wait_ge(s["base_in"][k], 16 * (half + 1 + s["half0"]))
                dve.wait_ge(s["sums_read"], b + 1 + s["block0"])
                link(dve.scalar_tensor_tensor(out=new_x[k][:], in0=new_x[k][:], scalar=st(k, 18), in1=base[k][:],
                                              op0=ALU.mult, op1=ALU.add))
                variance(link, new_x[k][:], k, s["var"])

            def wait_stores(s, stores, half, k):
                wait_past(dve, s["stored"][k], 16 * stores * half)

            def epilogue_h(s, half, k, per):
                b = 2 * half + k
                link = chained(s["chain2"], per * b + per - 1)
                relu_norm(link, new_x[k][:], k, lambda: dve.wait_ge(s["rstd"], b + 1), s["h_done"])

            def layer0(half, k):
                b = 2 * half + k
                for c in range(NCH):
                    weights_of = chunk_after(half, k, c, by=AHEAD + 2)
                    if weights_of and weights_of[2] == 0:
                        inverse_norm(*weights_of[:2])
                        incidence(*weights_of)
                    if after := chunk_after(half, k, c, by=AHEAD):
                        lo_part(s, stream(*after, ring=3), after[2])
                    if weights_of and weights_of[2] > 0:
                        incidence(*weights_of)
                    if c == 2 and not is_last(half, k):
                        degree_count(*following(half, k))
                    if not (isinstance(half, int) and b == 0):
                        if c == 1:
                            epilogue0_sums(*previous(half, k))
                        if c == 2:
                            epilogue0(*previous(half, k))
                        if c == 3:
                            epilogue_h(s, *previous(half, k), 6)

            degree_count(0, 0)
            inverse_norm(0, 0)
            for c in range(AHEAD + 2):
                incidence(0, 0, c)
            for c in range(AHEAD):
                lo_part(s, stream(0, 0, c, ring=3), c)
            blocks(dve, layer0)
            epilogue0_sums(*end)
            epilogue0(*end)

            s = phases[1]
            def prep1(half, k, tile):
                b = 2 * half + k
                dve.wait_ge(s["prep_hi"], b + 1 + s["block0"])
                dve.tensor_scalar(s_left[:, bass.ds(b, 1), 0], prep_b_ps[k][:, D:D + 1], 99.0, None, ALU.mult)
                dve.tensor_scalar(s_left[:, bass.ds(b, 1), 1], prep_b_ps[k][:, D:D + 1], -0.01, None, ALU.mult)
                dve.tensor_tensor(values[:, bass.ds(b, 1), 1, :].rearrange("p o d -> p (o d)"),
                                  values[:, bass.ds(b, 1), 1, :].rearrange("p o d -> p (o d)").bitcast(F32),
                                  values[:, bass.ds(b, 1), 0, :].rearrange("p o d -> p (o d)").bitcast(F32),
                                  ALU.subtract)
                dve.tensor_tensor(values2[:, bass.ds(b, 1), 1, :].rearrange("p o d -> p (o d)"),
                                  prep_b_ps[k][:, 0:D],
                                  values2[:, bass.ds(b, 1), 0, :].rearrange("p o d -> p (o d)").bitcast(F32),
                                  ALU.subtract).then_inc(s["prep_lo"], 1)

            prep_blocks(dve, prep1, [[lambda: epilogue_h(phases[0], *end, 6)]])

            def masked(half, k, c):
                b = 2 * half + k
                w = width(c)
                wait_adj(dve, s, half, k, c)
                dve.wait_ge(s["exp_done"], NCH * b + c + 1)
                dve.scalar_tensor_tensor(out=row[k][:, cols(c, w)], in0=row_in[k][:, cols(c, w)], scalar=0.0,
                                         in1=row[k][:, cols(c, w)], op0=ALU.not_equal, op1=ALU.mult,
                                         accum_out=part[k][:, 0, c:c + 1]).then_inc(s["ready"], 1)

            def left(half, k):
                dve.tensor_scalar(st(k, 26, 2), s_left[:, bass.ds(2 * half + k, 1), :]
                                  .rearrange("p o t -> p (o t)"), 1.0, None, ALU.mult).then_inc(s["left_here"], 1)

            dve.wait_ge(s["prep_lo"], NB + s["block0"])
            left(0, 0)
            for g in range(AHEAD):
                lo_part(s, stream(0, 0, g, GSTEPS, 3), g)

            PER1 = 14

            def sums1(half, k):
                b = 2 * half + k
                link = chained(s["chain2"], PER1 * b)
                dve.wait_ge(s["side_done"], b + 1 + s["block0"])
                dve.tensor_tensor(side2[k][:], sum_ps[k][:, 0:D], side[k][:], ALU.add).then_inc(s["ts_done"], 1)
                wait_stores(s, 2, half, k)
                dve.tensor_tensor(new_x[k][:], score_ps[k][:, 0:D], new_h[k][:], ALU.add).then_inc(s["sums_read"], 1)
                link(dve.tensor_reduce(st(k, 14), part[k][:, 0, :], AX.X, ALU.add))
                link(dve.tensor_scalar(st(k, 15), st(k, 14), 1e-5, None, ALU.add))
                link(dve.reciprocal(st(k, 16), st(k, 15)))

            def gates1(half, k):
                s = phases[1]
                b = 2 * half + k
                dve.wait_ge(s["mix_mm"], b + 1)
                link = chained(s["chain2"], PER1 * b + 3)
                link(dve.tensor_tensor(st(k, 0, 2), mix_ps[:, D:D + 2], gate_bias[:], ALU.add))
                dve.tensor_scalar(st(k, 0, 2), st(k, 0, 2), SIGMOID_FROM, None, ALU.max).then_inc(s["gate_arg"], 1)
                link(dve.tensor_tensor(side2[k][:], mix_ps[:, 0:D], bias_row[:], ALU.add))

            def mixed1(half, k):
                s = phases[1]
                b = 2 * half + k
                link = chained(s["chain2"], PER1 * b + 5)
                dve.wait_ge(s["gate_exp"], b + 1)
                link(dve.tensor_scalar(st(k, 20, 2), st(k, 2, 2), 1.0, None, ALU.add))
                link(dve.reciprocal(st(k, 22, 2), st(k, 20, 2)))
                link(dve.tensor_tensor(st(k, 24), st(k, 22), st(k, 16), ALU.mult))
                link(dve.tensor_scalar(side2[k][:], side2[k][:], st(k, 23), None, ALU.mult))
                dve.scalar_tensor_tensor(out=side2[k][:], in0=new_x[k][:], scalar=st(k, 24), in1=side2[k][:],
                                         op0=ALU.mult, op1=ALU.add).then_inc(s["sig_arg"], 1)

            def result1(half, k):
                s = phases[1]
                b = 2 * half + k
                link = chained(s["chain2"], PER1 * b + 9)
                dve.wait_ge(s["sig_tanh"], b + 1)
                dve.wait_ge(s["base_in"][k], 16 * (half + 1 + s["half0"]))
                link(dve.tensor_scalar(new_x[k][:], side[k][:], 0.5, 0.5, ALU.mult, ALU.add))
                link(dve.tensor_tensor(new_x[k][:], new_x[k][:], base[k][:], ALU.add))
                variance(link, new_x[k][:], k, s["var"])

            def layer1(half, k):
                b = 2 * half + k
                if not is_last(half, k):
                    left(*following(half, k))
                for g in range(GSTEPS):
                    if isinstance(half, int) and b == 0:
                        for c in (2 * g - 8, 2 * g - 7):
                            if 0 <= c < NCH:
                                masked(0, 0, c)
                    if g > NCH and not is_last(half, k):
                        masked(*following(half, k), g - NCH - 1)
                    if g == GSTEPS - 1 and not is_last(half, k):
                        masked(*following(half, k), NCH - 1)
                    if after := chunk_after(half, k, g, GSTEPS, AHEAD):
                        lo_part(s, stream(*after, GSTEPS, 3), after[2] % NCH)
                    if not (isinstance(half, int) and b == 0):
                        prev = previous(half, k)
                        if g == 1:
                            sums1(*prev)
                        if g == 5:
                            gates1(*prev)
                        if g == 6:
                            mixed1(*prev)
                        if g == 8:
                            result1(*prev)
                        if g == 10:
                            epilogue_h(s, *prev, PER1)

            blocks(dve, layer1)
            sums1(*end)

            for n in (2, 3, 4):
                s = phases[n]
                if n == 2:
                    dve.wait_ge(s["wts_in"], 3 * 16)

                def prep_with_bias(half, k, tile):
                    b = 2 * half + k
                    dve.wait_ge(s["prep_mm"], b + 1)
                    if not (isinstance(half, int) and b < 2):
                        dve.wait_ge(s["prep_lo"], b - 1 + s["block0"])
                    key_src, value_src = prep_fold[k]
                    dve.tensor_tensor(key_src, prep_a_ps[k].rearrange("p (c n) -> p c n", c=DC),
                                      bias_col[:, 1, :, None].broadcast_to((P, DC, P)), ALU.add)
                    dve.tensor_tensor(value_src, prep_b_ps[k][:, 0:D], value_bias, ALU.add)\
                       .then_inc(s["prep_fold"], 1)
                    if not (isinstance(half, int) and b == 0):
                        prep_lo_parts(*previous(half, k))

                def prep_lo_parts(half, k, tile=None):
                    b = 2 * half + k
                    if n == 2:
                        key_src, value_src = prep_fold[k]
                    else:
                        key_src = prep_a_ps[k].rearrange("p (c n) -> p c n", c=DC)
                        value_src = prep_b_ps[k][:, 0:D]
                    dve.wait_ge(s["prep_hi"], b + 1 + s["block0"])
                    dve.tensor_tensor(keys[:, :, 1, bass.ds(b * P, P)], key_src,
                                      keys[:, :, 0, bass.ds(b * P, P)].bitcast(F32), ALU.subtract)
                    dve.tensor_tensor(values[:, bass.ds(b, 1), 1, :].rearrange("p o d -> p (o d)"), value_src,
                                      values[:, bass.ds(b, 1), 0, :].rearrange("p o d -> p (o d)").bitcast(F32),
                                      ALU.subtract).then_inc(s["prep_lo"], 1)

                if n == 2:
                    tail = [[lambda: gates1(*end)], [lambda: mixed1(*end)], [lambda: result1(*end)],
                            [lambda: epilogue_h(phases[1], *end, PER1)]]
                elif n == 3:
                    tail = [[lambda: epilogue_h(phases[2], *end, 6)]]
                else:
                    tail = []
                prep_blocks(dve, prep_with_bias if n == 2 else prep_lo_parts, tail)
                if n == 2:
                    prep_lo_parts(*end)
                for k in range(2):
                    dve.memset(row[k][:, N:NP], 0.0)

                def query_fold_part(half, k):
                    b = 2 * half + k
                    dve.wait_ge(s["query_mm"], b + 1)
                    dve.tensor_tensor(fold[k][:], small_ps.rearrange("p (c n) -> p c n", c=DC),
                                      bias_col[:, 0, :, None].broadcast_to((P, DC, P)), ALU.add)\
                       .then_inc(s["query_fold"], 1)

                def query_lo_part(half, k):
                    b = 2 * half + k
                    dve.wait_ge(s["query_hi"], b + 1)
                    if n == 2:
                        dve.scalar_tensor_tensor(out=query_lo[k], in0=fold[k][:], scalar=1.0 / 32,
                                                 in1=query_hi[k].bitcast(F32), op0=ALU.mult,
                                                 op1=ALU.subtract).then_inc(s["query_lo"], 1)
                    else:
                        dve.tensor_tensor(query_lo[k], small_ps.rearrange("p (c n) -> p c n", c=DC),
                                          query_hi[k].bitcast(F32), ALU.subtract).then_inc(s["query_lo"], 1)

                def score_out(half, k, c):
                    b = 2 * half + k
                    j = (NCH * k + c) % 2
                    w = live(c)
                    dve.wait_ge(s["score_mm"], NCH * b + c + 1)
                    wait_past(dve, s["turned"], NCH * (b - 2) + c + 1)
                    top = part[k][:, 0, c:c + 1]
                    if n == 2:
                        wait_adj(dve, s, half, k, c)
                        take_wait(k, c)
                        dve.tensor_tensor_reduce(row[k][:, cols(c, w)], score_ps[j][:, 0:w],
                                                 row_in[k][:, cols(c, w)], 2.0, LOW, ALU.add, ALU.max, top)\
                           .then_inc(s["score_out"], 1)
                    else:
                        dve.tensor_scalar(row[k][:, cols(c, w)], score_ps[j][:, 0:w], 1.0, LOW, ALU.mult,
                                          ALU.max, accum_out=top).then_inc(s["score_out"], 1)

                def row_top(half, k):
                    b = 2 * half + k
                    dve.wait_ge(s["score_out"], NCH * (b + 1))
                    link = chained(s["chain"], b)
                    link(dve.tensor_reduce(st(k, 0), part[k][:, 0, :], AX.X, ALU.max))
                    dve.tensor_scalar(st(k, 1), st(k, 0), -1.0, None, ALU.mult).then_inc(s["top"], 1)

                def weigh(half, k, c):
                    b = 2 * half + k
                    w = live(c)
                    if n == 2:
                        return
                    dve.wait_ge(s["exp_done"], NCH * b + c + 1)
                    wait_adj(dve, s, half, k, c)
                    dve.tensor_tensor(row[k][:, cols(c, w)], row[k][:, cols(c, w)], row_in[k][:, cols(c, w)],
                                      ALU.mult).then_inc(s["ready"], 1)

                for k in range(2):
                    if n == 2:
                        query_fold_part(0, k)
                    query_lo_part(0, k)
                for c in range(NCH):
                    score_out(0, 0, c)
                row_top(0, 0)
                weigh(0, 0, 0)
                weigh(0, 0, 1)
                lo_part(s, stream(0, 0, 0), 0)

                def epilogue(half, k):
                    b = 2 * half + k
                    link = chained(s["chain2"], {2: 6, 3: 3, 4: 4}[n] * b)
                    link(dve.tensor_reduce(st(k, 17), part[k][:, 1, :], AX.X, ALU.add))
                    link(dve.reciprocal(st(k, 18), st(k, 17)))
                    dve.wait_ge(s["side_done"], b + 1 + s["block0"])
                    dve.wait_ge(s["base_in"][k], 16 * (half + 1 + s["half0"]))
                    if n < 4:
                        wait_stores(s, {2: 3, 3: 2}[n], half, k)
                    else:
                        wait_past(dve, out_stored[k], 16 * half)
                    dve.tensor_tensor(new_x[k][:], sum_ps[k][:, 0:D], side[k][:], ALU.add)\
                       .then_inc(s["sums_read"], 1)
                    dve.wait_ge(s["sums_read"], b + 1 + s["block0"])
                    link(dve.scalar_tensor_tensor(out=new_x[k][:], in0=new_x[k][:], scalar=st(k, 18),
                                                  in1=base[k][:], op0=ALU.mult, op1=ALU.add))
                    if n == 2:
                        variance(link, new_x[k][:], k, s["var"])
                        return
                    leaky = dve.scalar_tensor_tensor(out=new_x[k][:], in0=new_x[k][:], scalar=0.01,
                                                     in1=new_x[k][:], op0=ALU.mult, op1=ALU.max)
                    if n == 3:
                        leaky.then_inc(s["h_done"], 1)
                        return
                    link(leaky)
                    dve.wait_ge(s["extra_in"][k], 16 * (half + 1))
                    dve.tensor_tensor(new_x[k][:], new_x[k][:], side2[k][:], ALU.add).then_inc(s["h_out"], 1)

                def attend(half, k):
                    b = 2 * half + k
                    for c in range(NCH):
                        if not is_last(half, k):
                            for a in SCORES_AT[c]:
                                score_out(*following(half, k), a)
                            if NCH - 1 in SCORES_AT[c]:
                                row_top(*following(half, k))
                        if c + 2 < NCH:
                            weigh(half, k, c + 2)
                        elif not is_last(half, k):
                            weigh(*following(half, k), c + 2 - NCH)
                        if after := chunk_after(half, k, c):
                            lo_part(s, stream(*after), after[2])
                        if not (isinstance(half, int) and b == 0):
                            if c == 1:
                                epilogue(*previous(half, k))
                            if c == 3 and n == 2:
                                epilogue_h(s, *previous(half, k), 6)
                        if c == 5 and not (isinstance(half, int) and half == NB // 2 - 1):
                            if n == 2:
                                query_fold_part(half + 1, k)
                            query_lo_part(half + 1, k)

                blocks(dve, attend)
                epilogue(*end)

        @block.gpsimd
        def _(pool):
            pool.wait_ge(consts_set, 2)

            def rstd(arg, done):
                def slot(half, k):
                    pool.wait_ge(arg, 2 * half + k + 1)
                    nc.gpsimd.tensor_tensor(st(k, 13), st(k, 12), minus_half[:, 0:1], ALU.pow).then_inc(done, 1)

                return slot

            def stage(n):
                s = phases[n]

                def slot(half, k, tile):
                    b = 2 * half + k
                    if isinstance(half, int) and half == 0:
                        if n > 1:
                            pool.wait_ge(phases[n - 1]["mix_mm" if n == 2 else "query_mm"], NB - 1 + k)
                    else:
                        pool.wait_ge(s["prep_mm"], b - 1)
                    nc.gpsimd.tensor_tensor(spare[k][:, 0:1], minus_half[:, 0:1], minus_half[:, 0:1], ALU.add)
                    nc.gpsimd.tensor_copy(ht_in[k][:].rearrange("p c n -> p (c n)"),
                                          row[tile][:, bass.ds((b - tile * HALF_NB) * D, D)])\
                      .then_inc(s["stage_set"], 1)

                return slot

            def piece_here(n):
                return lambda i: pool.wait_ge(phases[n]["ht_piece"][i], 16 * n)

            s = phases[0]
            for i in range(2):
                of_i = slice(i * HALF_NB, (i + 1) * HALF_NB)
                pool.wait_ge(s["prep_var"], i + 1)
                nc.gpsimd.tensor_tensor(norm[:, of_i, 3], norm[:, of_i, 2], minus_half[:], ALU.pow)\
                  .then_inc(s["prep_rstd"], 1)

            def mask(half, k):
                b = 2 * half + k
                for c in range(MASKS_POOL):
                    wait_adj(pool, s, half, k, c)
                    wait_past(pool, s["turned"], NCH * (b - 2) + c + 1)
                    nc.gpsimd.tensor_tensor(spare[k][:, c:c + 1], minus_half[:, 0:1], minus_half[:, 0:1], ALU.add)
                    nc.gpsimd.tensor_scalar(row[k][:, cols(c, width(c))], row_in[k][:, cols(c, width(c))], 0.0, None,
                                            ALU.is_gt).then_inc(s["raw_done"], 1)

            def root(half, k):
                pool.wait_ge(s["inverse"], 2 * half + k + 1)
                nc.gpsimd.tensor_tensor(st(k, 15), st(k, 14), plus_half[:], ALU.pow).then_inc(s["root"], 1)

            norm0 = rstd(s["var"], s["rstd"])

            def layer0(half, k):
                if not is_last(half, k):
                    mask(*following(half, k))
                if not is_last(half, k):
                    root(*following(half, k))
                if not (isinstance(half, int) and 2 * half + k == 0):
                    norm0(*previous(half, k))

            mask(0, 0)
            root(0, 0)
            pool.wait_ge(phases[0]["prep_lo"], NB)
            blocks(pool, layer0)
            prep_blocks(pool, stage(1), [[], [lambda: norm0(*end)]], piece_here(1))

            s = phases[1]
            norm1 = rstd(s["var"], s["rstd"])

            def add_right(half, k):
                b = 2 * half + k
                for c in range(NCH):
                    pool.wait_ge(s["raw_done"], NCH * b + c + 1)
                    nc.gpsimd.tensor_tensor(row[k][:, cols(c, width(c))], row[k][:, cols(c, width(c))],
                                            s_right[:, cols(c, width(c))], ALU.add).then_inc(s["arg_done"], 1)

            def layer1(half, k):
                if not is_last(half, k):
                    add_right(*following(half, k))
                if not (isinstance(half, int) and 2 * half + k == 0):
                    norm1(*previous(half, k))

            add_right(0, 0)
            blocks(pool, layer1)
            prep_blocks(pool, stage(2), [[], [], [], [lambda: norm1(*end)]], piece_here(2))

            norm2 = rstd(phases[2]["var"], phases[2]["rstd"])

            def layer2(half, k):
                if not is_last(half, k):
                    norm2(half, k)

            blocks(pool, layer2)
            prep_blocks(pool, stage(3), [[], [lambda: norm2(*end)]], piece_here(3))
            prep_blocks(pool, stage(4), (), piece_here(4))


def kernel(x, adj, L1_gnn_W_sa, L1_gnn_a_sa, L1_gnn_W_gcnb, L1_gnn_b_gcnb, L1_gnn_Wa, L1_gnn_ba, L1_gnn_Wb,
           L1_gnn_bb, L2_gnn_Wq, L2_gnn_bq, L2_gnn_Wk, L2_gnn_bk, L2_gnn_Wv, L2_gnn_bv, L3_gnn_W_stack):
    import numpy as np
    import concourse.bacc as bacc
    from concourse.bass_utils import run_bass_kernel_spmd

    nc = bacc.Bacc("TRN2", target_bir_lowering=False, num_devices=1)

    def plain(a):
        return np.ascontiguousarray(np.asarray(a))

    x, adj = plain(x), plain(adj)
    x_pad = np.zeros((NP, D), x.dtype)
    x_pad[:N] = x
    x_pad[N:] = x[N - 1:]
    adj_pad = np.zeros((NP, NP), adj.dtype)
    adj_pad[:N, :N] = adj
    adj_pad[N:, :N] = adj[N - 1:]

    def on_all(a):
        return plain(np.tile(plain(a).reshape(1, -1), (P, 1)))

    def by_feature(a):
        return plain(plain(a).reshape(-1, P).T)

    arrays = {
        "in_x": x_pad.reshape(NB, P, D),
        "in_adj": adj_pad,
        "in_eye": np.eye(P, dtype=np.float32),
        "in_w_sa": plain(L1_gnn_W_sa),
        "in_a_sa": on_all(L1_gnn_a_sa),
        "in_w_gcnb": plain(L1_gnn_W_gcnb),
        "in_b_gcnb": on_all(L1_gnn_b_gcnb),
        "in_gate_w": plain(np.stack([by_feature(L1_gnn_Wa), by_feature(L1_gnn_Wb)], axis=1)),
        "in_gate_b": plain(np.concatenate([on_all(L1_gnn_ba), on_all(L1_gnn_bb)], axis=1)),
        "in_w_q": plain(plain(L2_gnn_Wq).T),
        "in_w_k": plain(plain(L2_gnn_Wk).T),
        "in_w_v": plain(plain(L2_gnn_Wv).T),
        "in_b_q": by_feature(L2_gnn_bq),
        "in_b_k": by_feature(L2_gnn_bk),
        "in_b_v": on_all(L2_gnn_bv),
        "in_w_stack": plain(L3_gnn_W_stack),
    }
    args = [nc.dram_tensor(name, a.shape, mybir.dt.from_np(a.dtype), kind="ExternalInput").ap()
            for name, a in arrays.items()]
    out = nc.dram_tensor("out", (NB, P, D), F32, kind="ExternalOutput").ap()
    graph_layers(nc, *args, out)
    result = run_bass_kernel_spmd(nc, [arrays], core_ids=[0])
    return result.results[0]["out"].reshape(NP, D)[:N]
```
